# Optimizing a Trainium2 kernel written in Bass

```python
import numpy as np
import jax
import jax.numpy as jnp

def _softmax(x, axis=-1):
    return jax.nn.softmax(x, axis=axis)

def _gelu(x):
    return jax.nn.gelu(x, approximate=True)

def _silu(x):
    return jax.nn.silu(x)

def _sigmoid(x):
    return jax.nn.sigmoid(x)

def _layernorm(x, axis=-1, eps=1e-05):
    m = jnp.mean(x, axis=axis, keepdims=True)
    v = jnp.var(x, axis=axis, keepdims=True)
    return (x - m) / jnp.sqrt(v + eps)

def _scatter_add(tgt, idx, src, axis=0):
    return tgt.at[idx].add(src)

def _segment_sum(src, seg, n):
    return jax.ops.segment_sum(src, seg, n)
kernel_name = 'mk_audio_tower_d1_tok_audfeat256_r4_e8a6c9'

def setup_inputs(seed: int=0):
    np.random.seed(seed)
    _w = jnp.asarray

    def _rec_inputs():
        import jax
        import jax.numpy as jnp
        _rk = jax.random.key(seed)
        x = -0.000520686 + 1.00062 * jax.random.normal(jax.random.fold_in(_rk, 1), (128, 375, 64), jnp.float32)
        return x
    x = _rec_inputs()

    def _L0_tok_setup():
        import jax, jax.numpy as jnp
        import numpy as np
        BATCH = 2
        SEQ = 1024
        D_MODEL = 64
        N_STATE = 64
        DT_RANK = 1
        NUM_LAYERS = 3

        def _ssm_layer(x, A_log, Dp, W_dbc, W_dt, b_dt):
            A = -jnp.exp(A_log)
            dbc = jnp.einsum('ble,ce->blc', x, W_dbc)
            delta, Bm, Cm = jnp.split(dbc, [DT_RANK, DT_RANK + N_STATE], axis=-1)
            delta = jax.nn.softplus(jnp.einsum('blr,er->ble', delta, W_dt) + b_dt)
            dA = jnp.exp(delta[..., None] * A)
            dBx = (delta * x)[..., None] * Bm[:, :, None, :]

            def combine(c1, c2):
                a1, h1 = c1
                a2, h2 = c2
                return (a1 * a2, h1 * a2 + h2)
            _, hs = jax.lax.associative_scan(combine, (dA, dBx), axis=1)
            y = jnp.einsum('blen,bln->ble', hs, Cm)
            return y + Dp * x
        key = jax.random.key(seed)
        kx, kw1, kw2 = jax.random.split(key, 3)
        x = jax.random.normal(kx, (BATCH, SEQ, D_MODEL), dtype=jnp.float32)
        A_log = jnp.broadcast_to(jnp.log(jnp.arange(1, N_STATE + 1, dtype=jnp.float32)), (NUM_LAYERS, D_MODEL, N_STATE)).copy()
        D = jnp.ones((NUM_LAYERS, D_MODEL), dtype=jnp.float32)
        W_dbc = 0.02 * jax.random.normal(kw1, (NUM_LAYERS, DT_RANK + 2 * N_STATE, D_MODEL), dtype=jnp.float32)
        W_dt = 0.02 * jax.random.normal(kw2, (NUM_LAYERS, D_MODEL, DT_RANK), dtype=jnp.float32)
        b_dt = jnp.zeros((NUM_LAYERS, D_MODEL), dtype=jnp.float32)
        return {'x': x, 'A_log': A_log, 'D': D, 'W_dbc': W_dbc, 'W_dt': W_dt, 'b_dt': b_dt}
    _L0_tok_all = _L0_tok_setup()
    _L0_tok_in = {k: v for k, v in _L0_tok_all.items() if k in ('A_log', 'D', 'W_dbc', 'W_dt', 'b_dt')}
    del _L0_tok_all

    def _L0_attn_setup():
        import jax, jax.numpy as jnp
        import numpy as np
        DIM = 64
        key = jax.random.key(seed)
        ks = jax.random.split(key, 7)
        x = jax.random.normal(ks[0], (4, 1024, DIM), dtype=jnp.float32)
        s = 1.0 / np.sqrt(DIM)
        Wq = jax.random.uniform(ks[1], (DIM, DIM), jnp.float32, -s, s)
        Wk = jax.random.uniform(ks[2], (DIM, DIM), jnp.float32, -s, s)
        Wv = jax.random.uniform(ks[3], (DIM, DIM), jnp.float32, -s, s)
        bq = jax.random.uniform(ks[4], (DIM,), jnp.float32, -s, s)
        bk = jax.random.uniform(ks[5], (DIM,), jnp.float32, -s, s)
        bv = jax.random.uniform(ks[6], (DIM,), jnp.float32, -s, s)
        return {'x': x, 'Wq': Wq, 'bq': bq, 'Wk': Wk, 'bk': bk, 'Wv': Wv, 'bv': bv}
    _L0_attn_all = _L0_attn_setup()
    _L0_attn_in = {k: v for k, v in _L0_attn_all.items() if k in ('Wq', 'bq', 'Wk', 'bk', 'Wv', 'bv')}
    del _L0_attn_all

    def _L0_ffn_setup():
        import jax, jax.numpy as jnp
        import numpy as np
        B, S, H, F, E, K = (8, 1024, 64, 128, 16, 2)
        EPS = 1e-05
        key = jax.random.key(seed)
        ks = jax.random.split(key, 9)
        sc = 0.02
        return {'x': jax.random.normal(ks[0], (B, S, H), dtype=jnp.float32), 'gate_w': jax.random.normal(ks[1], (H, E), dtype=jnp.float32) * sc, 'gate_b': jnp.zeros((E,), dtype=jnp.float32), 'w1': jax.random.normal(ks[2], (E, H, F), dtype=jnp.float32) * sc, 'b1': jnp.zeros((E, F), dtype=jnp.float32), 'w2': jax.random.normal(ks[3], (E, F, H), dtype=jnp.float32) * sc, 'b2': jnp.zeros((E, H), dtype=jnp.float32), 'gamma': jnp.ones((H,), dtype=jnp.float32), 'beta': jnp.zeros((H,), dtype=jnp.float32)}
    _L0_ffn_all = _L0_ffn_setup()
    _L0_ffn_in = {k: v for k, v in _L0_ffn_all.items() if k in ('gate_w', 'gate_b', 'w1', 'b1', 'w2', 'b2', 'gamma', 'beta')}
    del _L0_ffn_all
    return {'x': x, 'L0_tok_A_log': _L0_tok_in['A_log'], 'L0_tok_D': _L0_tok_in['D'], 'L0_tok_W_dbc': _L0_tok_in['W_dbc'], 'L0_tok_W_dt': _L0_tok_in['W_dt'], 'L0_tok_b_dt': _L0_tok_in['b_dt'], 'L0_attn_Wq': _L0_attn_in['Wq'], 'L0_attn_bq': _L0_attn_in['bq'], 'L0_attn_Wk': _L0_attn_in['Wk'], 'L0_attn_bk': _L0_attn_in['bk'], 'L0_attn_Wv': _L0_attn_in['Wv'], 'L0_attn_bv': _L0_attn_in['bv'], 'L0_ffn_gate_w': _L0_ffn_in['gate_w'], 'L0_ffn_gate_b': _L0_ffn_in['gate_b'], 'L0_ffn_w1': _L0_ffn_in['w1'], 'L0_ffn_b1': _L0_ffn_in['b1'], 'L0_ffn_w2': _L0_ffn_in['w2'], 'L0_ffn_b2': _L0_ffn_in['b2'], 'L0_ffn_gamma': _L0_ffn_in['gamma'], 'L0_ffn_beta': _L0_ffn_in['beta']}

def reference(x, L0_tok_A_log, L0_tok_D, L0_tok_W_dbc, L0_tok_W_dt, L0_tok_b_dt, L0_attn_Wq, L0_attn_bq, L0_attn_Wk, L0_attn_bk, L0_attn_Wv, L0_attn_bv, L0_ffn_gate_w, L0_ffn_gate_b, L0_ffn_w1, L0_ffn_b1, L0_ffn_w2, L0_ffn_b2, L0_ffn_gamma, L0_ffn_beta):
    import jax
    import jax.numpy as jnp

    def _L0_tok_ref(x, A_log, D, W_dbc, W_dt, b_dt):
        import jax, jax.numpy as jnp
        import numpy as np
        BATCH = 2
        SEQ = 1024
        D_MODEL = 64
        N_STATE = 64
        DT_RANK = 1
        NUM_LAYERS = 3

        def _ssm_layer(x, A_log, Dp, W_dbc, W_dt, b_dt):
            A = -jnp.exp(A_log)
            dbc = jnp.einsum('ble,ce->blc', x, W_dbc)
            delta, Bm, Cm = jnp.split(dbc, [DT_RANK, DT_RANK + N_STATE], axis=-1)
            delta = jax.nn.softplus(jnp.einsum('blr,er->ble', delta, W_dt) + b_dt)
            dA = jnp.exp(delta[..., None] * A)
            dBx = (delta * x)[..., None] * Bm[:, :, None, :]

            def combine(c1, c2):
                a1, h1 = c1
                a2, h2 = c2
                return (a1 * a2, h1 * a2 + h2)
            _, hs = jax.lax.associative_scan(combine, (dA, dBx), axis=1)
            y = jnp.einsum('blen,bln->ble', hs, Cm)
            return y + Dp * x
        for i in range(NUM_LAYERS):
            x = _ssm_layer(x, A_log[i], D[i], W_dbc[i], W_dt[i], b_dt[i])
            if i < NUM_LAYERS - 1:
                b, l, d = x.shape
                x = x[:, :l // 2 * 2].reshape(b, l // 2, 2, d).mean(axis=2)
        return x

    def _L0_attn_ref(x, Wq, bq, Wk, bk, Wv, bv):
        import jax, jax.numpy as jnp
        import numpy as np
        DIM = 64
        q = jnp.einsum('bsd,ed->bse', x, Wq) + bq
        k = jnp.einsum('bsd,ed->bse', x, Wk) + bk
        v = jnp.einsum('bsd,ed->bse', x, Wv) + bv
        scale = 1.0 / jnp.sqrt(jnp.float32(x.shape[-1]))
        scores = jnp.einsum('bse,bte->bst', q, k) * scale
        weights = jax.nn.softmax(scores, axis=-1)
        return jnp.einsum('bst,bte->bse', weights, v)

    def _L0_ffn_ref(x, gate_w, gate_b, w1, b1, w2, b2, gamma, beta):
        import jax, jax.numpy as jnp
        import numpy as np
        B, S, H, F, E, K = (8, 1024, 64, 128, 16, 2)
        EPS = 1e-05
        gate_logits = x @ gate_w + gate_b
        topk_vals, topk_idx = jax.lax.top_k(gate_logits, K)
        topk_w = jax.nn.softmax(topk_vals, axis=-1)
        h = jax.nn.relu(jnp.einsum('bsh,ehf->bsef', x, w1) + b1)
        expert_out = jnp.einsum('bsef,efh->bseh', h, w2) + b2
        sel = jnp.take_along_axis(expert_out, topk_idx[:, :, :, None], axis=2)
        moe = jnp.sum(topk_w[..., None] * sel, axis=2)
        y = x + moe
        mu = jnp.mean(y, axis=-1, keepdims=True)
        var = jnp.var(y, axis=-1, keepdims=True)
        return (y - mu) / jnp.sqrt(var + EPS) * gamma + beta
    h = _L0_tok_ref(x, L0_tok_A_log, L0_tok_D, L0_tok_W_dbc, L0_tok_W_dt, L0_tok_b_dt)
    h = h + _L0_attn_ref(_layernorm(h, axis=-1), L0_attn_Wq, L0_attn_bq, L0_attn_Wk, L0_attn_bk, L0_attn_Wv, L0_attn_bv)
    h = h + _L0_ffn_ref(_layernorm(h, axis=-1), L0_ffn_gate_w, L0_ffn_gate_b, L0_ffn_w1, L0_ffn_b1, L0_ffn_w2, L0_ffn_b2, L0_ffn_gamma, L0_ffn_beta)
    return h

_drawn_inputs = setup_inputs


def setup_inputs(seed=0):
    import zlib

    import numpy as np

    out = dict(_drawn_inputs(seed))
    spreads = {'L0_tok_D': (1.0, 0.2),
     'L0_tok_b_dt': (0.0, 0.644),
     'L0_ffn_gate_b': (0.0, 0.1),
     'L0_ffn_b1': (0.0, 0.8),
     'L0_ffn_b2': (0.0, 0.1),
     'L0_ffn_gamma': (1.0, 0.2),
     'L0_ffn_beta': (0.0, 0.1)}
    factors = {'L0_tok_A_log': 5.978,
     'L0_tok_W_dt': 23.773,
     'L0_attn_bq': 5.358,
     'L0_attn_bk': 64.0,
     'L0_ffn_w1': 5.673,
     'L0_ffn_w2': 4.239}
    for name, (base, spread) in spreads.items():
        noise = np.random.default_rng([zlib.crc32(name.encode()), seed]).standard_normal(out[name].shape)
        drawn = base * np.exp(spread * noise) if base else spread * noise
        out[name] = jnp.asarray(drawn.astype(out[name].dtype))
    for name, factor in factors.items():
        out[name] = (out[name] * factor).astype(out[name].dtype)
    return out
```

```python
from contextlib import ExitStack

import numpy as np
import concourse.bass as bass
from concourse import mybir

F32 = mybir.dt.float32
BF16 = mybir.dt.bfloat16
ACT = mybir.ActivationFunctionType
ALU = mybir.AluOpType
AX = mybir.AxisListType

BATCH, SEQ, D, NST, LAYERS = 128, 375, 64, 64, 3
PAIRS = BATCH // 2
LEN3 = (SEQ // 2) // 2
LENS = [4 * LEN3, 2 * LEN3, LEN3]
N = 4 * LEN3
GROUPS = [PAIRS, PAIRS // 2, PAIRS // 4]
FIRST = [0, PAIRS, PAIRS + PAIRS // 2]
TOTAL = sum(GROUPS)
CH = 16
BANK = 512
SPLITS = 3
AROWS = SPLITS * SPLITS * 2
DXROWS = SPLITS * 2
DX0 = AROWS + 1
QUARTERS = 4

SMALL_U = 5.6e-3
RESET = -1e4
LAG = 4
KR = 128


def ssm_stage(nc, ctx, io):
    def sb(name, shape, dt=F32):
        return ctx.enter_context(nc.sbuf_tensor(name, shape, dt))

    def ps(name, shape, dt=F32):
        return ctx.enter_context(nc.psum_tensor(name, shape, dt))

    def sem(name):
        return ctx.enter_context(nc.semaphore(name))

    x1, x2, x3, y3 = io["x"], io["x2"], io["x3"], io["y3"]
    parts_dram = io["parts_dram"]

    w_a = [sb(f"w_a{i}", [128, D, 2, NST], BF16) for i in range(LAYERS)]
    w_dx = sb("w_dx", [128, 2, NST], BF16)
    rhs = sb("rhs", [128, CH, 4, N], BF16)
    w_z = [sb(f"w_z{i}", [128, 128]) for i in range(LAYERS)]
    w_b = [sb(f"w_b{i}", [128, 128]) for i in range(LAYERS)]
    w_c = [sb(f"w_c{i}", [128, 128]) for i in range(LAYERS)]
    w_d = [sb(f"w_d{i}", [128, 128]) for i in range(LAYERS)]
    bias_dt = sb("bias_dt", [128, LAYERS])
    sel = sb("sel", [128, CH, 32])
    sel_half = sb("sel_half", [128, CH, 32])

    psA = ps("psA", [128, 2, BANK])
    psX = [ps(f"psX{i}", [128, 2, BANK]) for i in range(2)]
    psY = ps("psY", [128, BANK])
    psM = ps("psM", [128, BANK])

    s = {k: sem(k) for k in (
        "setup_in", "setup_v", "setup_s", "setup_g", "setup_st", "setup_w",
        "x_in0", "x_in1", "rhs_in0", "rhs_in1", "rhs_in2", "rhs_in3", "parts_out", "y_out",
        "pa_full", "exp_done", "px_full", "dbx_done", "scan_done", "hc_done", "red_done",
        "skip_done", "evac_done", "z_ready", "z_used", "b_ready", "b_done", "c_ready", "c_done",
        "m_a", "m_v", "m_g", "m_p")}

    outer, ctx = ctx, ExitStack()
    apart = sb("apart", [64, SPLITS, 2, 2, NST], BF16)
    arest = sb("arest", [64, NST])
    araw = sb("araw", [64, LAYERS, NST])
    aexp = sb("aexp", [64, NST])
    w0col = sb("w0col", [128, LAYERS])
    dcol = sb("dcol", [128, LAYERS])
    wdt_row = sb("wdt_row", [128, LAYERS, 128])
    wb_raw = sb("wb_raw", [128, LAYERS, 128])
    wc_raw = sb("wc_raw", [128, LAYERS, 128])
    mask_z = sb("mask_z", [128, 128])
    mask_n = sb("mask_n", [128, 128])
    ident = sb("ident", [128, 128])

    with nc.Block() as block:
        @block.sync
        def _(sp):
            for dst, src in ((w0col, "w0"), (dcol, "dcol"), (bias_dt, "bdt"), (wb_raw, "wb"), (wc_raw, "wc"),
                             (mask_z, "mask_z"), (mask_n, "mask_n"), (ident, "ident"), (sel, "sel")):
                sp.dma_start(dst[:], io[src]).then_inc(s["setup_in"], 16)
            sp.dma_start(wdt_row[:], io["wdt"].partition_broadcast(128)).then_inc(s["setup_in"], 16)
            sp.dma_start(araw[:], io["A_log"].rearrange("l e n -> e l n")).then_inc(s["setup_in"], 16)
            sp.wait_ge(s["setup_g"], LAYERS + 2)
            sp.dma_start(w_dx[DX0:DX0 + DXROWS, :, :], io["ones_dx"]).then_inc(s["setup_w"], 16)
            for i in range(LAYERS):
                sp.wait_ge(s["setup_v"], 10 * i + 10)
                a_dram = io["a_dram"][i]
                sp.dma_start(a_dram.rearrange("j b e m -> e j b m"),
                             apart[:].rearrange("e j b c n -> e j b (c n)")).then_inc(s["setup_st"], 16)
                sp.wait_ge(s["setup_st"], 16 * (i + 1))
                for j in range(SPLITS):
                    for q in range(SPLITS):
                        r = 6 * j + 2 * q
                        sp.dma_start(w_a[i][r:r + 2, :, :, :].rearrange("r e c n -> r (e c n)"),
                                     a_dram[j].rearrange("b e m -> b (e m)")).then_inc(s["setup_w"], 16)
                sp.dma_start(w_a[i][AROWS:AROWS + 1, :, :, :].rearrange("r e c n -> r (e c n)"),
                             io["ones_row"]).then_inc(s["setup_w"], 16)
            sp.wait_ge(s["setup_w"], 16 * (1 + LAYERS * 10))

        @block.gpsimd
        def _(pool):
            for i in range(LAYERS):
                nc.gpsimd.memset(w_a[i][:].rearrange("p e c n -> p (e c n)").bitcast(F32), 0.0).then_inc(s["setup_g"], 1)
            nc.gpsimd.memset(w_dx[:], 0.0).then_inc(s["setup_g"], 1)
            nc.gpsimd.memset(rhs[:].rearrange("p c r n -> p (c r n)").bitcast(F32), 0.0).then_inc(s["setup_g"], 1)

        @block.scalar
        def _(act):
            act.wait_ge(s["setup_in"], 16 * 11)
            for i in range(LAYERS):
                if i > 0:
                    act.wait_ge(s["setup_v"], 10 * i)
                nc.scalar.activation(aexp[:], araw[:, i, :], ACT.Exp).then_inc(s["setup_s"], 1)

        @block.vector
        def _(dve):
            v = nc.vector
            done = [0]

            def step(ins):
                done[0] += 1
                ins.then_inc(s["setup_v"], 1)
                dve.wait_ge(s["setup_v"], done[0])
            dve.wait_ge(s["setup_in"], 16 * 11)
            for i in range(LAYERS):
                if i > 0:
                    dve.wait_ge(s["setup_st"], 16 * i)
                step(v.memset(apart[:], 0.0))
                dve.wait_ge(s["setup_s"], i + 1)
                step(v.tensor_scalar(arest[:], aexp[:], 1e36, -1.0, ALU.min, ALU.mult))
                for j in range(SPLITS):
                    step(v.tensor_copy(apart[:, j, 0, 0, :], arest[:]))
                    if j < SPLITS - 1:
                        step(v.tensor_tensor(arest[:], arest[:], apart[:, j, 0, 0, :], ALU.subtract))
                    else:
                        step(v.tensor_copy(apart[:, :, 1, 1, :], apart[:, :, 0, 0, :]))
                step(v.tensor_scalar(w_z[i][:], wdt_row[:, i, :], w0col[:, i:i + 1], None, ALU.mult))
                step(v.tensor_tensor(w_z[i][:], w_z[i][:], mask_z[:], ALU.mult))
            for i in range(LAYERS):
                v.tensor_tensor(w_b[i][:], wb_raw[:, i, :], mask_n[:], ALU.mult)
                v.tensor_tensor(w_c[i][:], wc_raw[:, i, :], mask_n[:], ALU.mult)
                v.tensor_scalar(w_d[i][:], ident[:], dcol[:, i:i + 1], 1.0 if i == LAYERS - 1 else 0.5,
                                ALU.mult, ALU.mult)
            v.tensor_scalar(sel_half[:], sel[:], 0.5, None, ALU.mult)

    ctx.close()
    ctx = outer

    xin = sb("xin", [128, 2, N])
    proj_b = sb("proj_b", [128, 2, N])
    proj_c = sb("proj_c", [128, 2, N])
    az = sb("az", [128, N])
    relu_z = sb("relu_z", [128, N])
    u = sb("u", [128, N])
    t = sb("t", [128, N])
    lnw = sb("lnw", [128, N])
    small = sb("small", [128, N])
    dd = sb("dd", [128, 2, N])
    rest = sb("rest", [128, 2, N])
    parts = sb("parts", [128, 2, SPLITS, N], BF16)
    dA = sb("dA", [128, 2, 4, N])
    dBx = sb("dBx", [128, 4, 4, N])
    hst = sb("hst", [128, 4, 4, N])
    hc = sb("hc", [128, 2, 4, N])
    yt = sb("yt", [128, 2, N])

    dst_of = [x2, x3, None]
    src_of = [x1, x2, x3]

    def count(g, per, c):
        layer, k = g
        return k * per + (FIRST[layer] * per + c)

    def positive(v):
        return not isinstance(v, int) or v > 0

    def parity_count(g, par, per):
        layer, k = g
        return (k - par) * (per // 2) + (FIRST[layer] * (per // 2) + per)

    def groups(eng, emit):
        def nth(n):
            if n < 0 or n >= TOTAL:
                return None
            layer = max(i for i in range(LAYERS) if n >= FIRST[i])
            return (layer, n - FIRST[layer])
        for layer in range(LAYERS):
            G = GROUPS[layer]

            def static(k):
                n = FIRST[layer] + k
                emit(nth(n), n % 2, nth(n - 1), nth(n + 1), nth(n + 2))
            static(0)
            static(1)
            with eng.Fori(1, G // 2 - 1) as i:
                for j in range(2):
                    emit(*((layer, i * 2 + (j + d)) if d is not None else j for d in (0, None, -1, 1, 2)))
            static(G - 2)
            static(G - 1)
        return nth(TOTAL - 1)

    def bcast_e(ap, m):
        return ap.unsqueeze(1).to_broadcast([128, m, N])

    with nc.Block() as block:
        @block.sync
        def _(sp):
            def load_x(g, par, reader=None):
                layer, k = g
                G = 1 << layer
                src = src_of[layer][bass.ds(k * G, G), :, :].rearrange("g p l -> p g l")
                if reader is not None:
                    sp.wait_ge(s["skip_done"], count(reader, 1, 1))
                if layer > 0:
                    sp.wait_ge(s["y_out"], count((layer - 1, k * 2), 16, 32))
                sp.dma_start(xin[:, par, :].rearrange("p (g l) -> p g l", g=G), src).then_inc(s[f"x_in{par}"], 16)

            def store_parts(g, par):
                sp.wait_ge(s["m_g"], count(g, 2, 2))
                for r in range(4):
                    for b in range(2):
                        sp.dma_start(parts_dram[par, :, b, :, r, :].rearrange("q c n -> c q n"),
                                     parts[32 * r + b:32 * r + 32:2, :, :, :].rearrange("p a q n -> p (a q) n")
                                     ).then_inc(s["parts_out"], 16)
                sp.wait_ge(s["parts_out"], count(g, 128, 128))

            def load_rhs(g, par):
                layer, _ = g
                for q in range(QUARTERS):
                    c0, c1 = q * CH // QUARTERS, (q + 1) * CH // QUARTERS
                    arrived = s[f"rhs_in{q}"]
                    if positive(count(g, 32, 2 * c1 - 32)):
                        sp.wait_ge(s["pa_full"], count(g, 32, 2 * c1 - 32))

                    def rows(r, n):
                        return rhs[r:r + n, c0:c1, :, :].rearrange("r c k n -> r (c k n)")
                    def piece(ap):
                        return ap[:, c0:c1, :, :].rearrange("r c k n -> r (c k n)")
                    pd = parts_dram[par].rearrange("q b c k n -> (q b) c k n")
                    for j in range(SPLITS):
                        sp.dma_start(rows(DXROWS * j, DXROWS), piece(pd[0:DXROWS])).then_inc(arrived, 16)
                    sp.dma_start(rows(AROWS, 1), piece(io["reset_rows"][layer:layer + 1])).then_inc(arrived, 16)
                    sp.dma_start(rows(DX0, DXROWS), piece(pd[DXROWS:2 * DXROWS])).then_inc(arrived, 16)

            def store_y(g, par):
                layer, k = g
                if layer == LAYERS - 1:
                    dst = y3[bass.ds(k, 1), :, :].rearrange("g p l -> p (g l)")
                    src = yt[:, par, :]
                else:
                    G = 1 << layer
                    dst = dst_of[layer][bass.ds(k * G, G), :, :].rearrange("g p l -> p g l")
                    src = yt[:, par, 0:N // 2].rearrange("p (g l) -> p g l", g=G)
                sp.wait_ge(s["evac_done"], count(g, 1, 1))
                sp.dma_start(dst, src).then_inc(s["y_out"], 16)

            def emit(g, par, before, nxt, nxt2):
                if before is not None:
                    store_y(before, 1 - par)
                if nxt2 is not None:
                    load_x(nxt2, par, g)
                if nxt is not None:
                    store_parts(nxt, 1 - par)
                    load_rhs(nxt, 1 - par)

            load_x((0, 0), 0)
            load_x((0, 1), 1)
            store_parts((0, 0), 0)
            load_rhs((0, 0), 0)
            last = groups(sp, emit)
            store_y(last, 1)
            sp.wait_ge(s["y_out"], count(last, 16, 16))

        def pe_compact(pe, g, par, c):
            layer, _ = g
            def proj(w):
                return nc.tensor.matmul(psM[:, 0:N], w[layer][:], xin[:, par, :], start=True, stop=True)
            if c == 2:
                pe.wait_ge(s[f"x_in{par}"], parity_count(g, par, 16))
                if positive(count(g, 1, 0)):
                    pe.wait_ge(s["c_done"], count(g, 1, 0))
                proj(w_z).then_inc(s["z_ready"], 1)
            if c == 4:
                pe.wait_ge(s["m_a"], count(g, 7, 2))
                proj(w_b).then_inc(s["b_ready"], 1)
            if c == 6:
                pe.wait_ge(s["b_done"], count(g, 1, 1))
                proj(w_c).then_inc(s["c_ready"], 1)

        def act_compact(act, g, par, c):
            layer, _ = g
            a = nc.scalar.activation
            if c == 2:
                act.wait_ge(s["z_ready"], count(g, 1, 1))
                a(az[:], psM[:, 0:N], ACT.Abs, bias=bias_dt[:, layer:layer + 1]).then_inc(s["m_a"], 1)
                a(relu_z[:], psM[:, 0:N], ACT.Relu, bias=bias_dt[:, layer:layer + 1]).then_inc(s["m_a"], 1)
            if c == 3:
                act.wait_ge(s["m_a"], count(g, 7, 1))
                a(u[:], az[:], ACT.Exp, scale=-1.0).then_inc(s["m_a"], 1)
                act.wait_ge(s["m_a"], count(g, 7, 3))
                a(t[:], u[:], ACT.Copy, bias=1.0, scale=-0.5).then_inc(s["m_a"], 1)
                a(lnw[:], u[:], ACT.Ln, bias=1.0).then_inc(s["m_a"], 1)
            if c == 4:
                act.wait_ge(s["b_ready"], count(g, 1, 1))
                a(proj_b[:, par, :], psM[:, 0:N], ACT.Copy).then_inc(s["b_done"], 1)
            if c == 6:
                act.wait_ge(s["c_ready"], count(g, 1, 1))
                a(proj_c[:, par, :], psM[:, 0:N], ACT.Copy).then_inc(s["c_done"], 1)
            if c == 8:
                act.wait_ge(s["m_v"], count(g, 5, 5))
                a(parts[:, :, 0, :], dd[:], ACT.Copy).then_inc(s["m_a"], 1)
            if c == 11:
                act.wait_ge(s["m_g"], count(g, 2, 1))
                a(parts[:, :, 1, :], rest[:], ACT.Copy).then_inc(s["m_a"], 1)

        def dve_compact(dve, g, par, c):
            v = nc.vector
            if c == 4:
                dve.wait_ge(s["m_a"], count(g, 7, 5))
                v.scalar_tensor_tensor(lnw[:], u[:], SMALL_U, lnw[:], ALU.is_ge, ALU.mult).then_inc(s["m_v"], 1)
                v.tensor_tensor(small[:], t[:], u[:], ALU.mult).then_inc(s["m_v"], 1)
            if c == 5:
                dve.wait_ge(s["m_v"], count(g, 5, 2))
                v.tensor_tensor(lnw[:], lnw[:], small[:], ALU.max).then_inc(s["m_v"], 1)
            if c == 6:
                dve.wait_ge(s["m_v"], count(g, 5, 3))
                v.tensor_tensor(dd[:, 0, :], lnw[:], relu_z[:], ALU.add).then_inc(s["m_v"], 1)
            if c == 7:
                dve.wait_ge(s["m_v"], count(g, 5, 4))
                v.tensor_tensor(dd[:, 1, :], dd[:, 0, :], xin[:, par, :], ALU.mult).then_inc(s["m_v"], 1)

        def pool_compact(pool, g, par, c):
            p = nc.gpsimd
            if c == 6:
                pool.wait_ge(s["m_a"], count(g, 7, 6))
                p.tensor_tensor(rest[:], dd[:], parts[:, :, 0, :], ALU.subtract).then_inc(s["m_g"], 1)
            if c == 9:
                pool.wait_ge(s["m_a"], count(g, 7, 7))
                p.tensor_tensor(parts[:, :, 2, :], rest[:], parts[:, :, 1, :],
                                ALU.subtract).then_inc(s["m_g"], 1)

        @block.tensor
        def _(pe):
            mm = nc.tensor.matmul

            def spread_dx(g, c, hf):
                if c % (CH // QUARTERS) == 0 and hf == 0:
                    pe.wait_ge(s[f"rhs_in{c * QUARTERS // CH}"], count(g, 80, 80))
                if positive(count(g, 32, 2 * c + hf - 1)):
                    pe.wait_ge(s["dbx_done"], count(g, 32, 2 * c + hf - 1))
                for q in range(2):
                    ins = mm(psX[hf][:, q, 0:N], w_dx[0:KR], rhs[0:KR, c, 2 * hf + q, :], start=True, stop=True)
                ins.then_inc(s["px_full"], 1)

            def spread_a(g, c, hf):
                layer, _ = g
                if positive(count(g, 32, 2 * c + hf)):
                    pe.wait_ge(s["exp_done"], count(g, 32, 2 * c + hf))
                for q in range(2):
                    e = c + CH * (2 * hf + q)
                    ins = mm(psA[:, q, 0:N], w_a[layer][0:KR, e, :, :], rhs[0:KR, c, 2 * hf + q, :],
                             start=True, stop=True)
                ins.then_inc(s["pa_full"], 1)

            def reduce(g, par, c):
                layer, _ = g
                weights = sel if layer == LAYERS - 1 else sel_half
                if c == 0:
                    if positive(count(g, 1, 0)):
                        pe.wait_ge(s["evac_done"], count(g, 1, 0))
                    mm(psY[:, 0:N], w_d[layer][:], xin[:, par, :], start=True, stop=False,
                       skip_group_check=True).then_inc(s["skip_done"], 1)
                pe.wait_ge(s["hc_done"], count(g, 16, c + 1))
                for r in range(4):
                    ins = mm(psY[32 * r:32 * r + 32, 0:N], weights[:, c, :], hc[:, c % 2, r, :],
                             start=False, stop=c == CH - 1, skip_group_check=True)
                ins.then_inc(s["red_done"], 1)

            def emit(g, par, before, nxt, nxt2):
                for c in range(CH):
                    for hf in range(2):
                        spread_dx(g, c, hf)
                        if c > 0:
                            spread_a(g, c - 1, hf)
                        elif before is not None:
                            spread_a(before, CH - 1, hf)
                        if hf == 1:
                            continue
                        if c >= LAG:
                            reduce(g, par, c - LAG)
                        elif before is not None:
                            reduce(before, 1 - par, CH + c - LAG)
                    if nxt is not None:
                        pe_compact(pe, nxt, 1 - par, c)

            for c in range(CH):
                pe_compact(pe, (0, 0), 0, c)
            last = groups(pe, emit)
            for hf in range(2):
                spread_a(last, CH - 1, hf)
            for c in range(CH - LAG, CH):
                reduce(last, 1, c)

        @block.scalar
        def _(act):
            def decay(g, c):
                if positive(count(g, 16, c - 1)):
                    act.wait_ge(s["scan_done"], count(g, 16, c - 1))
                for hf in range(2):
                    act.wait_ge(s["pa_full"], count(g, 32, 2 * c + hf + 1))
                    nc.scalar.activation(dA[:, c % 2, 2 * hf:2 * hf + 2, :], psA[:, :, 0:N],
                                         ACT.Exp).then_inc(s["exp_done"], 1)

            def emit(g, par, before, nxt, nxt2):
                for c in range(CH):
                    if c > 0:
                        decay(g, c - 1)
                    elif before is not None:
                        decay(before, CH - 1)
                    if nxt is not None:
                        act_compact(act, nxt, 1 - par, c)

            for c in range(CH):
                act_compact(act, (0, 0), 0, c)
            last = groups(act, emit)
            decay(last, CH - 1)

        @block.vector
        def _(dve):
            v = nc.vector

            def scan(g, c):
                dve.wait_ge(s["exp_done"], count(g, 32, 2 * c + 2))
                dve.wait_ge(s["dbx_done"], count(g, 32, 2 * c + 2))
                if positive(count(g, 16, c - 3)):
                    dve.wait_ge(s["hc_done"], count(g, 16, c - 3))
                v.tensor_tensor_scan(hst[:, c % 4, :, :].rearrange("p e n -> p (e n)"),
                                     dA[:, c % 2, :, :].rearrange("p e n -> p (e n)"),
                                     dBx[:, c % 4, :, :].rearrange("p e n -> p (e n)"),
                                     0.0, ALU.mult, ALU.add).then_inc(s["scan_done"], 1)

            def evac(g, par):
                layer, _ = g
                dve.wait_ge(s["red_done"], count(g, 16, 16))
                if layer == LAYERS - 1:
                    v.tensor_copy(yt[:, par, :], psY[:, 0:N]).then_inc(s["evac_done"], 1)
                else:
                    v.tensor_reduce(yt[:, par, 0:N // 2], psY[:, 0:N].rearrange("p (l two) -> p l two", two=2),
                                    AX.X, ALU.add).then_inc(s["evac_done"], 1)

            def emit(g, par, before, nxt, nxt2):
                for c in range(CH):
                    if positive(count(g, 16, c - 3)):
                        dve.wait_ge(s["scan_done"], count(g, 16, c - 3))
                    for hf in range(2):
                        if c == 0 and hf == 0:
                            dve.wait_ge(s["b_done"], count(g, 1, 1))
                        dve.wait_ge(s["px_full"], count(g, 32, 2 * c + hf + 1))
                        v.tensor_tensor(dBx[:, c % 4, 2 * hf:2 * hf + 2, :], psX[hf][:, :, 0:N],
                                        bcast_e(proj_b[:, par, :], 2), ALU.mult).then_inc(s["dbx_done"], 1)
                    if c == LAG - 1 and before is not None:
                        evac(before, 1 - par)
                    if c > 0:
                        scan(g, c - 1)
                    elif before is not None:
                        scan(before, CH - 1)
                    if nxt is not None:
                        dve_compact(dve, nxt, 1 - par, c)

            for c in range(CH):
                dve_compact(dve, (0, 0), 0, c)
            last = groups(dve, emit)
            scan(last, CH - 1)
            evac(last, 1)

        @block.gpsimd
        def _(pool):
            def emit(g, par, before, nxt, nxt2):
                for c in range(CH):
                    if c == 0:
                        pool.wait_ge(s["c_done"], count(g, 1, 1))
                    pool.wait_ge(s["scan_done"], count(g, 16, c + 1))
                    if positive(count(g, 16, c - 1)):
                        pool.wait_ge(s["red_done"], count(g, 16, c - 1))
                    nc.gpsimd.tensor_tensor(hc[:, c % 2, :, :], hst[:, c % 4, :, :],
                                            bcast_e(proj_c[:, par, :], 4), ALU.mult).then_inc(s["hc_done"], 1)
                    if nxt is not None:
                        pool_compact(pool, nxt, 1 - par, c)

            for c in range(CH):
                pool_compact(pool, (0, 0), 0, c)
            groups(pool, emit)


LT = LEN3
GP = 4
SEQS = 2 * GP
E_FFN, F_FFN = 16, 128
EPS = 1e-5
V_STEPS = 39


def attention_ffn_stage(nc, io, out):
    with ExitStack() as ctx:
        def sb(name, shape, dt=F32):
            return ctx.enter_context(nc.sbuf_tensor(name, shape, dt))

        def ps(name, shape, dt=F32):
            return ctx.enter_context(nc.psum_tensor(name, shape, dt))

        sems = {}

        def sem(name):
            if name not in sems:
                sems[name] = ctx.enter_context(nc.semaphore("f_" + name))
            return sems[name]

        w = {n: sb("f_" + n, list(io[n].shape)) for n in (
            "wq_t", "wk_t", "wv_t", "gate_t", "bq_c", "bk_c", "w1_t", "b1_t", "w2_t", "b2_t", "ident", "halves",
            "halves_g", "halves_b", "order")}
        rows = {n: sb("f_" + n, [LT, io[n].shape[1]]) for n in ("bv_r", "gateb_r", "gamma_r", "beta_r")}
        eps_c = sb("f_eps", [128, 1])

        feat = sb("f_feat", [128, N])
        hid = sb("f_hid", [LT, 2, GP, D])
        cen = sb("f_cen", [LT, 2, GP, D])
        sq = sb("f_sq", [LT, 2, GP, D])
        stat = sb("f_stat", [LT, 4, SEQS])
        xn = sb("f_xn", [LT, GP, 2, D])
        xn_t = sb("f_xn_t", [128, N])
        q_t = sb("f_q_t", [128, N])
        k_t = sb("f_k_t", [128, N])
        val = sb("f_val", [LT, GP, 2, D])
        peak = sb("f_peak", [LT, 2, GP])
        prob = sb("f_prob", [LT, 2, GP, LT])
        prob_t = sb("f_prob_t", [LT, 2, N])
        den = sb("f_den", [LT, 2, 2, GP])
        att = sb("f_att", [LT, 2, GP, D])
        hid2 = sb("f_hid2", [LT, 2, GP, D])
        logit = sb("f_logit", [LT, SEQS, E_FFN])
        pick = sb("f_pick", [LT, 2, SEQS, E_FFN])
        code = sb("f_code", [LT, SEQS, E_FFN])
        top = sb("f_top", [LT, 6, SEQS])
        gates = sb("f_gates", [LT, SEQS, E_FFN])
        gates_t = sb("f_gates_t", [2 * E_FFN, N])
        hidden = sb("f_hidden", [128, 2, 2, N])
        scaled = sb("f_scaled", [LT, 2, SEQS, D])
        acc = sb("f_acc", [LT, SEQS, D])
        res = sb("f_res", [LT, 2, GP, D])

        pT = ps("f_pT", [128, BANK])
        pB = ps("f_pB", [128, BANK])
        pH = ps("f_pH", [128, 2, BANK])
        pF = [ps(f"f_pF{i}", [128, BANK]) for i in range(2)]
        pE = ps("f_pE", [128, BANK])
        pG = ps("f_pG", [128, BANK])

        with nc.Block() as block:
            @block.sync
            def _(sp):
                for n, tile in {**w, **rows}.items():
                    src = io[n] if n in w else io[n].partition_broadcast(LT).rearrange("p a c -> p (a c)")
                    sp.dma_start(tile[:], src).then_inc(sem("weights"), 16)
                sp.wait_ge(sem("weights"), 16 * (len(w) + len(rows)))

            @block.vector
            def _(dve):
                nc.vector.memset(eps_c[:], EPS).then_inc(sem("eps"), 1)
                dve.wait_ge(sem("weights"), 16 * (len(w) + len(rows)))
                for n in ("wq_t", "wk_t", "wv_t"):
                    nc.vector.tensor_tensor(w[n][:], w[n][:], w["halves"][:], ALU.mult).then_inc(sem("masked"), 1)
                nc.vector.tensor_tensor(w["gate_t"][:], w["gate_t"][:], w["halves_g"][:],
                                        ALU.mult).then_inc(sem("masked"), 1)
                nc.vector.tensor_tensor(w["b2_t"][:], w["b2_t"][:], w["halves_b"][:],
                                        ALU.mult).then_inc(sem("masked"), 1)

        def each(eng, emit):
            with eng.Fori(0, GROUPS[-1]) as k:
                emit(k)
                eng.wait_ge(sem("stored"), k * 32 + 32)

        def wide(ap, n):
            return ap.unsqueeze(3).to_broadcast([LT, ap.shape[1], ap.shape[2], n])

        with nc.Block() as block:
            @block.sync
            def _(sp):
                def emit(k):
                    src = io["y3"][bass.ds(k, 1), :, :].rearrange("a p n -> p (a n)")
                    dst = out[bass.ds(k * SEQS, SEQS), :, :].rearrange("(g b) l e -> b l g e", b=2)
                    if not isinstance(k, int):
                        sp.wait_ge(sem("stored"), k * 32)
                    sp.dma_start(feat[:], src).then_inc(sem("feat"), 16)
                    sp.wait_ge(sem("res"), k + 1)
                    for b in range(2):
                        sp.dma_start(dst[b], res[:, b, :, :]).then_inc(sem("stored"), 16)
                emit(0)
                with sp.Fori(1, GROUPS[-1]) as k:
                    emit(k)
                sp.wait_ge(sem("stored"), 32 * GROUPS[-1])

            @block.tensor
            def _(pe):
                mm, tr = nc.tensor.matmul, nc.tensor.transpose
                ident = w["ident"]

                def to_features(name, k, c):
                    pe.wait_ge(sem("xn"), k * 3 + c)
                    for g in range(GP):
                        ins = tr(pB[:, g * LT:(g + 1) * LT], xn[:, g, :, :].rearrange("p b e -> p (b e)"),
                                 ident[0:LT, 0:LT])
                    ins.then_inc(sem(name), 1)

                def emit(k):
                    pe.wait_ge(sem("feat"), k * 16 + 16)
                    for g in range(GP):
                        ins = tr(pT[0:LT, g * 128:(g + 1) * 128], feat[:, g * LT:(g + 1) * LT], ident[:])
                    ins.then_inc(sem("tokens"), 1)
                    to_features("xn_ps", k, 1)
                    pe.wait_ge(sem("xn_t"), k * 2 + 1)
                    mm(pH[:, 0, 0:N], w["wq_t"][:], xn_t[:], start=True, stop=True)
                    mm(pH[:, 1, 0:N], w["wk_t"][:], xn_t[:], start=True, stop=True).then_inc(sem("qk_ps"), 1)
                    for g in range(GP):
                        ins = mm(pE[0:LT, g * 128:(g + 1) * 128], xn_t[:, g * LT:(g + 1) * LT], w["wv_t"][:],
                                 start=True, stop=True)
                    ins.then_inc(sem("v_ps"), 1)
                    pe.wait_ge(sem("qk"), k * 2 + 2)
                    for b in range(2):
                        for g in range(GP):
                            cols = slice(g * LT, (g + 1) * LT)
                            ins = mm(pH[0:LT, b, cols], q_t[64 * b:64 * b + 64, cols], k_t[64 * b:64 * b + 64, cols],
                                     start=True, stop=True)
                    ins.then_inc(sem("scores"), 1)
                    pe.wait_ge(sem("prob"), k + 1)
                    for b in range(2):
                        for g in range(GP):
                            ins = tr(pF[b][0:LT, g * LT:(g + 1) * LT], prob[:, b, g, :], ident[0:LT, 0:LT])
                    ins.then_inc(sem("prob_ps"), 1)
                    pe.wait_ge(sem("prob_t"), k * 2 + 2)
                    pe.wait_ge(sem("val"), k + 1)
                    for b in range(2):
                        for g in range(GP):
                            j = b * GP + g
                            ins = mm(pE[0:LT, j * D:(j + 1) * D], prob_t[:, b, g * LT:(g + 1) * LT], val[:, g, b, :],
                                     start=True, stop=True)
                    ins.then_inc(sem("att_ps"), 1)
                    to_features("xn2_ps", k, 2)
                    pe.wait_ge(sem("xn_t"), k * 2 + 2)
                    for g in range(GP):
                        ins = mm(pG[0:LT, g * 32:(g + 1) * 32], xn_t[:, g * LT:(g + 1) * LT], w["gate_t"][:],
                                 start=True, stop=True)
                    ins.then_inc(sem("logit_ps"), 1)

                    def second(x):
                        pe.wait_ge(sem("hidden"), k * E_FFN + (x + 1))
                        if x >= 2:
                            pe.wait_ge(sem("scaled"), k * E_FFN + (x - 1))
                        for g in range(GP):
                            for b in range(2):
                                j = 2 * g + b
                                ins = mm(pF[x % 2][0:LT, j * D:(j + 1) * D],
                                         hidden[:, x % 2, b, g * LT:(g + 1) * LT], w["w2_t"][:, x, :],
                                         start=True, stop=True)
                        ins.then_inc(sem("expert_ps"), 1)
                    for b in range(2):
                        ins = mm(pH[:, b, 0:N], w["w1_t"][64 * b:64 * b + 64, 0, :], xn_t[64 * b:64 * b + 64, :],
                                 start=True, stop=True)
                    ins.then_inc(sem("hidden_ps"), 1)
                    for x in range(E_FFN):
                        if x + 1 < E_FFN:
                            pe.wait_ge(sem("hidden"), k * E_FFN + (x + 1))
                            for b in range(2):
                                ins = mm(pH[:, b, 0:N], w["w1_t"][64 * b:64 * b + 64, x + 1, :],
                                         xn_t[64 * b:64 * b + 64, :], start=True, stop=True)
                            ins.then_inc(sem("hidden_ps"), 1)
                        second(x)
                    pe.wait_ge(sem("gates"), k + 1)
                    for g in range(GP):
                        ins = tr(pT[0:2 * E_FFN, g * LT:(g + 1) * LT],
                                 gates[:, 2 * g:2 * g + 2, :].rearrange("p b x -> p (b x)"), ident[0:LT, 0:LT])
                    ins.then_inc(sem("gates_ps"), 1)
                    pe.wait_ge(sem("gates_t"), k + 1)
                    for g in range(GP):
                        ins = mm(pE[0:LT, g * 128:(g + 1) * 128], gates_t[:, g * LT:(g + 1) * LT], w["b2_t"][:],
                                 start=True, stop=True)
                    ins.then_inc(sem("bias2_ps"), 1)
                each(pe, emit)

            @block.scalar
            def _(act):
                a = nc.scalar.activation

                def rstd(k, c):
                    act.wait_ge(sem("var"), k * 3 + c)
                    a(stat[:, 2, :], stat[:, 1, :], ACT.Ln, bias=eps_c[0:LT, :], scale=1.0 / D
                      ).then_inc(sem("ln_var"), 1)
                    act.wait_ge(sem("ln_var"), k * 3 + c)
                    a(stat[:, 3, :], stat[:, 2, :], ACT.Exp, scale=-0.5).then_inc(sem("rstd"), 1)

                def emit(k):
                    rstd(k, 1)
                    act.wait_ge(sem("xn_ps"), k + 1)
                    a(xn_t[:], pB[:, 0:N], ACT.Copy).then_inc(sem("xn_t"), 1)
                    act.wait_ge(sem("qk_ps"), k + 1)
                    a(q_t[:], pH[:, 0, 0:N], ACT.Identity, bias=w["bq_c"][:, 0:1]).then_inc(sem("qk"), 1)
                    a(k_t[:], pH[:, 1, 0:N], ACT.Identity, bias=w["bk_c"][:, 0:1]).then_inc(sem("qk"), 1)
                    act.wait_ge(sem("shifted"), k + 1)
                    a(prob[:], prob[:], ACT.Exp, scale=float(D) ** -0.5).then_inc(sem("prob"), 1)
                    act.wait_ge(sem("prob_ps"), k + 1)
                    for b in range(2):
                        a(prob_t[:, b, :], pF[b][0:LT, 0:N], ACT.Copy).then_inc(sem("prob_t"), 1)
                    rstd(k, 2)
                    act.wait_ge(sem("xn2_ps"), k + 1)
                    a(xn_t[:], pB[:, 0:N], ACT.Copy).then_inc(sem("xn_t"), 1)
                    act.wait_ge(sem("gap"), k + 1)
                    a(top[:, 4, :], top[:, 2, :], ACT.Exp).then_inc(sem("ratio"), 1)
                    for x in range(E_FFN):
                        act.wait_ge(sem("hidden_ps"), k * E_FFN + (x + 1))
                        if x >= 2:
                            act.wait_ge(sem("expert_ps"), k * E_FFN + (x - 1))
                        a(hidden[:, x % 2, :, :], pH[:, :, 0:N], ACT.Relu, bias=w["b1_t"][:, x:x + 1]
                          ).then_inc(sem("hidden"), 1)
                    act.wait_ge(sem("gates_ps"), k + 1)
                    a(gates_t[:], pT[0:2 * E_FFN, 0:N], ACT.Copy).then_inc(sem("gates_t"), 1)
                    rstd(k, 3)
                each(act, emit)

            @block.vector
            def _(dve):
                v = nc.vector

                def emit(k):
                    steps = [0]

                    def then(ins):
                        steps[0] += 1
                        ins.then_inc(sem("v_step"), 1)
                        dve.wait_ge(sem("v_step"), k * V_STEPS + steps[0])

                    def norm(src, c):
                        then(v.tensor_reduce(stat[:, 0, :], src, AX.X, ALU.add))
                        then(v.tensor_scalar(stat[:, 0, :], stat[:, 0, :], 1.0 / D, None, ALU.mult))
                        mean = wide(stat[:, 0, :].rearrange("p (b g) -> p b g", b=2), D)
                        then(v.tensor_tensor(cen[:], src, mean, ALU.subtract))
                        then(v.tensor_tensor(sq[:], cen[:], cen[:], ALU.mult))
                        v.tensor_reduce(stat[:, 1, :], sq[:], AX.X, ALU.add).then_inc(sem("var"), 1)
                        dve.wait_ge(sem("rstd"), k * 3 + c)
                        v.tensor_tensor(xn[:].rearrange("p g b e -> p b g e"), cen[:],
                                        wide(stat[:, 3, :].rearrange("p (b g) -> p b g", b=2), D),
                                        ALU.mult).then_inc(sem("xn"), 1)

                    dve.wait_ge(sem("tokens"), k + 1)
                    then(v.tensor_copy(hid[:], pT[0:LT, :].rearrange("p (g e b) -> p b g e", g=GP, b=2)))
                    norm(hid[:], 1)
                    dve.wait_ge(sem("v_ps"), k + 1)
                    v.tensor_tensor(val[:].rearrange("p g b e -> p g (b e)"),
                                    pE[0:LT, :].rearrange("p (g m) -> p g m", g=GP),
                                    rows["bv_r"][:].unsqueeze(1).to_broadcast([LT, GP, 128]),
                                    ALU.add).then_inc(sem("val"), 1)
                    dve.wait_ge(sem("scores"), k + 1)
                    s4 = pH[0:LT, :, 0:N].rearrange("p b (g t) -> p b g t", g=GP)
                    then(v.tensor_reduce(peak[:], s4, AX.X, ALU.max))
                    v.tensor_tensor(prob[:], s4, wide(peak[:], LT), ALU.subtract).then_inc(sem("shifted"), 1)
                    dve.wait_ge(sem("prob"), k + 1)
                    then(v.tensor_reduce(den[:, 0, :, :], prob[:], AX.X, ALU.add))
                    then(v.reciprocal(den[:, 1, :, :], den[:, 0, :, :]))
                    dve.wait_ge(sem("att_ps"), k + 1)
                    then(v.tensor_tensor(att[:], pE[0:LT, :].rearrange("p (b g e) -> p b g e", b=2, g=GP),
                                         wide(den[:, 1, :, :], D), ALU.mult))
                    then(v.tensor_tensor(hid2[:], hid[:], att[:], ALU.add))
                    norm(hid2[:], 2)
                    dve.wait_ge(sem("logit_ps"), k + 1)
                    lg = logit[:]
                    then(v.tensor_tensor(lg.rearrange("p (g b) x -> p g (b x)", g=GP),
                                         pG[0:LT, 0:GP * 32].rearrange("p (g m) -> p g m", g=GP),
                                         rows["gateb_r"][:].unsqueeze(1).to_broadcast([LT, GP, 32]), ALU.add))

                    def over(ap):
                        return ap.unsqueeze(2).to_broadcast([LT, SEQS, E_FFN])
                    order = w["order"][0:LT, :].unsqueeze(1).to_broadcast([LT, SEQS, E_FFN])
                    for i in range(2):
                        then(v.tensor_reduce(top[:, i, :], lg, AX.X, ALU.max))
                        then(v.tensor_tensor(code[:], lg, over(top[:, i, :]), ALU.is_equal))
                        then(v.tensor_tensor(code[:], code[:], order, ALU.mult))
                        then(v.tensor_reduce(top[:, 5, :], code[:], AX.X, ALU.max))
                        then(v.tensor_tensor(pick[:, i, :, :], code[:], over(top[:, 5, :]), ALU.is_equal))
                        if i == 0:
                            then(v.tensor_scalar(code[:], pick[:, 0, :, :], -3e38, None, ALU.mult))
                            then(v.tensor_tensor(lg, lg, code[:], ALU.add))
                    v.tensor_tensor(top[:, 2, :], top[:, 1, :], top[:, 0, :], ALU.subtract).then_inc(sem("gap"), 1)
                    dve.wait_ge(sem("ratio"), k + 1)
                    then(v.tensor_scalar(top[:, 5, :], top[:, 4, :], 1.0, None, ALU.add))
                    then(v.reciprocal(top[:, 2, :], top[:, 5, :]))
                    then(v.tensor_tensor(top[:, 3, :], top[:, 4, :], top[:, 2, :], ALU.mult))
                    then(v.tensor_tensor(gates[:], pick[:, 0, :, :], over(top[:, 2, :]), ALU.mult))
                    then(v.tensor_tensor(code[:], pick[:, 1, :, :], over(top[:, 3, :]), ALU.mult))
                    v.tensor_tensor(gates[:], gates[:], code[:], ALU.add).then_inc(sem("gates"), 1)
                    dve.wait_ge(sem("gates"), k + 1)
                    for x in range(E_FFN):
                        dve.wait_ge(sem("expert_ps"), k * E_FFN + (x + 1))
                        if x >= 2:
                            dve.wait_ge(sem("summed"), k * E_FFN + (x - 1))
                        v.tensor_tensor(scaled[:, x % 2, :, :],
                                        pF[x % 2][0:LT, :].rearrange("p (j e) -> p j e", j=SEQS),
                                        gates[:, :, x:x + 1].to_broadcast([LT, SEQS, D]),
                                        ALU.mult).then_inc(sem("scaled"), 1)
                    dve.wait_ge(sem("summed"), k * E_FFN + E_FFN)
                    dve.wait_ge(sem("bias2_ps"), k + 1)
                    then(v.tensor_tensor(hid[:].rearrange("p b g e -> p g b e"),
                                         acc[:].rearrange("p (g b) e -> p g b e", g=GP),
                                         pE[0:LT, :].rearrange("p (g b e) -> p g b e", g=GP, b=2), ALU.add))
                    norm(hid[:], 3)
                    dve.wait_ge(sem("xn"), k * 3 + 3)
                    then(v.tensor_tensor(att[:].rearrange("p b g e -> p (b g) e"),
                                         xn[:].rearrange("p g b e -> p (g b) e"),
                                         rows["gamma_r"][:].unsqueeze(1).to_broadcast([LT, SEQS, D]), ALU.mult))
                    then(v.tensor_tensor(cen[:].rearrange("p b g e -> p (b g) e"),
                                         att[:].rearrange("p b g e -> p (b g) e"),
                                         rows["beta_r"][:].unsqueeze(1).to_broadcast([LT, SEQS, D]), ALU.add))
                    v.tensor_tensor(res[:].rearrange("p b g e -> p g b e"),
                                    cen[:].rearrange("p b g e -> p (b g e)").rearrange("p (g b e) -> p g b e", g=GP, b=2),
                                    hid2[:].rearrange("p b g e -> p g b e"), ALU.add).then_inc(sem("res"), 1)
                    return steps[0]

                
                with dve.Fori(0, GROUPS[-1]) as k:
                    n = emit(k)
                    assert n == V_STEPS, n
                    dve.wait_ge(sem("stored"), k * 32 + 32)

            @block.gpsimd
            def _(pool):
                def emit(k):
                    for x in range(E_FFN):
                        pool.wait_ge(sem("scaled"), k * E_FFN + (x + 1))
                        if x > 0:
                            pool.wait_ge(sem("summed"), k * E_FFN + x)
                        nc.gpsimd.tensor_tensor(acc[:], xn[:].rearrange("p g b e -> p (g b) e") if x == 0 else acc[:],
                                                scaled[:, x % 2, :, :], ALU.add).then_inc(sem("summed"), 1)
                each(pool, emit)


def tower(nc, io, out):
    with ExitStack() as ctx:
        ssm_stage(nc, ctx, io)
    attention_ffn_stage(nc, io, out)


def _layouts(inputs):
    f32, bf16 = np.float32, mybir.dt.np(BF16)
    lane = np.arange(128)
    channel, seq = lane // 2, lane % 2
    seq_s, state = lane // 64, lane % 64
    x = inputs["x"][:, :N].reshape(PAIRS, 2, N, D).transpose(0, 3, 1, 2).reshape(PAIRS, 128, N)
    w_dbc = inputs["L0_tok_W_dbc"]
    got = {
        "x": x, "w0": w_dbc[:, 0, :][:, channel].T, "dcol": inputs["L0_tok_D"][:, channel].T,
        "bdt": inputs["L0_tok_b_dt"][:, channel].T,
        "wb": w_dbc[:, 1:1 + NST, :][:, state][:, :, channel].transpose(2, 0, 1),
        "wc": w_dbc[:, 1 + NST:, :][:, state][:, :, channel].transpose(2, 0, 1),
        "wdt": inputs["L0_tok_W_dt"][:, channel, 0], "A_log": inputs["L0_tok_A_log"],
        "bq_c": inputs["L0_attn_bq"][state][:, None], "bk_c": inputs["L0_attn_bk"][state][:, None],
        "bv_r": inputs["L0_attn_bv"][state][None], "gateb_r": inputs["L0_ffn_gate_b"][np.arange(32) % 16][None],
        "gamma_r": inputs["L0_ffn_gamma"][None], "beta_r": inputs["L0_ffn_beta"][None],
        "gate_t": inputs["L0_ffn_gate_w"][state][:, np.arange(32) % 16],
        "w1_t": inputs["L0_ffn_w1"].transpose(1, 0, 2)[state], "b1_t": inputs["L0_ffn_b1"].T,
        "w2_t": inputs["L0_ffn_w2"].transpose(1, 0, 2), "b2_t": inputs["L0_ffn_b2"][np.arange(32) % 16][:, state],
    }
    for n in "qkv":
        got[f"w{n}_t"] = inputs[f"L0_attn_W{n}"].T[state][:, state]
    got["mask_z"] = np.equal.outer(seq, seq).astype(f32)
    got["mask_n"] = np.equal.outer(seq, seq_s).astype(f32)
    got["halves"] = np.equal.outer(seq_s, seq_s).astype(f32)
    got["halves_g"] = np.equal.outer(seq_s, np.arange(32) // 16).astype(f32)
    got["halves_b"] = np.equal.outer(np.arange(32) // 16, seq_s).astype(f32)
    got["ident"] = np.eye(128, dtype=f32)
    got["order"] = np.tile(np.arange(16, 0, -1, dtype=f32), (128, 1))
    sel = np.zeros((128, CH, 32), f32)
    for c in range(CH):
        sel[:64, c, 2 * c] = 1
        sel[64:, c, 2 * c + 1] = 1
    got["sel"] = sel
    ones_dx = np.zeros((DXROWS, 2, NST), bf16)
    for r in range(DXROWS):
        ones_dx[r, r % 2] = 1
    got["ones_dx"] = ones_dx
    got["ones_row"] = np.ones((1, D * 2 * NST), bf16)
    reset = np.zeros((LAYERS, CH, 4, N), bf16)
    for i, length in enumerate(LENS):
        reset[i, :, :, ::length] = RESET
    got["reset_rows"] = reset
    return got


def kernel(**inputs):
    import concourse.bacc as _bacc
    from concourse.bass_utils import run_bass_kernel_spmd as _run

    nc = _bacc.Bacc("TRN2", target_bir_lowering=False, num_devices=1)
    arrays, io = {}, {}
    for name, a in _layouts({k: np.asarray(v) for k, v in inputs.items()}).items():
        a = np.ascontiguousarray(a)
        arrays[f"in_{name}_dram"] = a
        io[name] = nc.dram_tensor(f"in_{name}_dram", a.shape, mybir.dt.from_np(a.dtype), kind="ExternalInput").ap()
    for name, shape, dt in (("x2", [PAIRS, 128, N // 2], F32), ("x3", [PAIRS, 128, N // 4], F32),
                            ("y3", [GROUPS[-1], 128, N], F32), ("a_dram", [LAYERS, SPLITS, 2, D, 2 * NST], BF16),
                            ("parts_dram", [2, 2 * SPLITS, 2, CH, 4, N], BF16)):
        io[name] = nc.dram_tensor(f"{name}_dram", shape, dt).ap()
    out = nc.dram_tensor("out_dram", [BATCH, LEN3, D], F32, kind="ExternalOutput").ap()
    tower(nc, io, out)
    r = _run(nc, [arrays], core_ids=[0])
    return r.results[0]["out_dram"]
```

```python
from contextlib import ExitStack

import numpy as np
import concourse.bass as bass
from concourse import mybir

F32 = mybir.dt.float32
BF16 = mybir.dt.bfloat16
ACT = mybir.ActivationFunctionType
ALU = mybir.AluOpType
AX = mybir.AxisListType

BATCH, SEQ, D, NST, LAYERS = 128, 375, 64, 64, 3
PAIRS = BATCH // 2
LEN3 = (SEQ // 2) // 2
LENS = [4 * LEN3, 2 * LEN3, LEN3]
N = 4 * LEN3
GROUPS = [PAIRS, PAIRS // 2, PAIRS // 4]
FIRST = [0, PAIRS, PAIRS + PAIRS // 2]
TOTAL = sum(GROUPS)
CH = 16
BANK = 512
SPLITS = 3
AROWS = SPLITS * SPLITS * 2
DXROWS = SPLITS * 2
DX0 = AROWS + 1
QUARTERS = 4

SMALL_U = 5.6e-3
RESET = -1e4
LAG = 4
KR = 128


def ssm_stage(nc, ctx, io):
    def sb(name, shape, dt=F32):
        return ctx.enter_context(nc.sbuf_tensor(name, shape, dt))

    def ps(name, shape, dt=F32):
        return ctx.enter_context(nc.psum_tensor(name, shape, dt))

    def sem(name):
        return ctx.enter_context(nc.semaphore(name))

    x1, x2, x3, y3 = io["x"], io["x2"], io["x3"], io["y3"]
    parts_dram = io["parts_dram"]

    w_a = [sb(f"w_a{i}", [128, D, 2, NST], BF16) for i in range(LAYERS)]
    w_dx = sb("w_dx", [128, 2, NST], BF16)
    rhs = sb("rhs", [128, CH, 4, N], BF16)
    w_z = [sb(f"w_z{i}", [128, 128]) for i in range(LAYERS)]
    w_b = [sb(f"w_b{i}", [128, 128]) for i in range(LAYERS)]
    w_c = [sb(f"w_c{i}", [128, 128]) for i in range(LAYERS)]
    w_d = [sb(f"w_d{i}", [128, 128]) for i in range(LAYERS)]
    bias_dt = sb("bias_dt", [128, LAYERS])
    sel = sb("sel", [128, CH, 32])
    

    psA = ps("psA", [128, 2, BANK])
    psX = [ps(f"psX{i}", [128, 2, BANK]) for i in range(2)]
    psY = ps("psY", [128, BANK])
    psM = ps("psM", [128, BANK])

    s = {k: sem(k) for k in (
        "setup_in", "setup_v", "setup_s", "setup_g", "setup_st", "setup_w",
        "x_in0", "x_in1", "rhs_in0", "rhs_in1", "rhs_in2", "rhs_in3", "parts_out", "y_out",
        "pa_full", "exp_done", "px_full", "dbx_done", "scan_done", "hc_done", "red_done",
        "skip_done", "evac_done", "z_ready", "z_used", "b_ready", "b_done", "c_ready", "c_done",
        "m_a", "m_v", "m_g", "m_p")}

    outer, ctx = ctx, ExitStack()
    apart = sb("apart", [64, SPLITS, 2, 2, NST], BF16)
    arest = sb("arest", [64, NST])
    araw = sb("araw", [64, LAYERS, NST])
    aexp = sb("aexp", [64, NST])
    w0col = sb("w0col", [128, LAYERS])
    dcol = sb("dcol", [128, LAYERS])
    wdt_row = sb("wdt_row", [128, LAYERS, 128])
    wb_raw = sb("wb_raw", [128, LAYERS, 128])
    wc_raw = sb("wc_raw", [128, LAYERS, 128])
    mask_z = sb("mask_z", [128, 128])
    mask_n = sb("mask_n", [128, 128])
    ident = sb("ident", [128, 128])

    with nc.Block() as block:
        @block.sync
        def _(sp):
            for dst, src in ((w0col, "w0"), (dcol, "dcol"), (bias_dt, "bdt"), (wb_raw, "wb"), (wc_raw, "wc"),
                             (mask_z, "mask_z"), (mask_n, "mask_n"), (ident, "ident"), (sel, "sel")):
                sp.dma_start(dst[:], io[src]).then_inc(s["setup_in"], 16)
            sp.dma_start(wdt_row[:], io["wdt"].partition_broadcast(128)).then_inc(s["setup_in"], 16)
            sp.dma_start(araw[:], io["A_log"].rearrange("l e n -> e l n")).then_inc(s["setup_in"], 16)
            sp.wait_ge(s["setup_g"], LAYERS + 2)
            sp.dma_start(w_dx[DX0:DX0 + DXROWS, :, :], io["ones_dx"]).then_inc(s["setup_w"], 16)
            for i in range(LAYERS):
                sp.wait_ge(s["setup_v"], 10 * i + 10)
                a_dram = io["a_dram"][i]
                sp.dma_start(a_dram.rearrange("j b e m -> e j b m"),
                             apart[:].rearrange("e j b c n -> e j b (c n)")).then_inc(s["setup_st"], 16)
                sp.wait_ge(s["setup_st"], 16 * (i + 1))
                for j in range(SPLITS):
                    for q in range(SPLITS):
                        r = 6 * j + 2 * q
                        sp.dma_start(w_a[i][r:r + 2, :, :, :].rearrange("r e c n -> r (e c n)"),
                                     a_dram[j].rearrange("b e m -> b (e m)")).then_inc(s["setup_w"], 16)
                sp.dma_start(w_a[i][AROWS:AROWS + 1, :, :, :].rearrange("r e c n -> r (e c n)"),
                             io["ones_row"]).then_inc(s["setup_w"], 16)
            sp.wait_ge(s["setup_w"], 16 * (1 + LAYERS * 10))

        @block.gpsimd
        def _(pool):
            for i in range(LAYERS):
                nc.gpsimd.memset(w_a[i][:].rearrange("p e c n -> p (e c n)").bitcast(F32), 0.0).then_inc(s["setup_g"], 1)
            nc.gpsimd.memset(w_dx[:], 0.0).then_inc(s["setup_g"], 1)
            nc.gpsimd.memset(rhs[:].rearrange("p c r n -> p (c r n)").bitcast(F32), 0.0).then_inc(s["setup_g"], 1)

        @block.scalar
        def _(act):
            act.wait_ge(s["setup_in"], 16 * 11)
            for i in range(LAYERS):
                if i > 0:
                    act.wait_ge(s["setup_v"], 10 * i)
                nc.scalar.activation(aexp[:], araw[:, i, :], ACT.Exp).then_inc(s["setup_s"], 1)

        @block.vector
        def _(dve):
            v = nc.vector
            done = [0]

            def step(ins):
                done[0] += 1
                ins.then_inc(s["setup_v"], 1)
                dve.wait_ge(s["setup_v"], done[0])
            dve.wait_ge(s["setup_in"], 16 * 11)
            for i in range(LAYERS):
                if i > 0:
                    dve.wait_ge(s["setup_st"], 16 * i)
                step(v.memset(apart[:], 0.0))
                dve.wait_ge(s["setup_s"], i + 1)
                step(v.tensor_scalar(arest[:], aexp[:], 1e36, -1.0, ALU.min, ALU.mult))
                for j in range(SPLITS):
                    step(v.tensor_copy(apart[:, j, 0, 0, :], arest[:]))
                    if j < SPLITS - 1:
                        step(v.tensor_tensor(arest[:], arest[:], apart[:, j, 0, 0, :], ALU.subtract))
                    else:
                        step(v.tensor_copy(apart[:, :, 1, 1, :], apart[:, :, 0, 0, :]))
                step(v.tensor_scalar(w_z[i][:], wdt_row[:, i, :], w0col[:, i:i + 1], None, ALU.mult))
                step(v.tensor_tensor(w_z[i][:], w_z[i][:], mask_z[:], ALU.mult))
            for i in range(LAYERS):
                v.tensor_tensor(w_b[i][:], wb_raw[:, i, :], mask_n[:], ALU.mult)
                v.tensor_tensor(w_c[i][:], wc_raw[:, i, :], mask_n[:], ALU.mult)
                v.tensor_scalar(w_d[i][:], ident[:], dcol[:, i:i + 1], 0.5,
                                ALU.mult, ALU.mult)
            v.tensor_scalar(sel[:], sel[:], 0.5, None, ALU.mult)

    ctx.close()
    ctx = outer

    xin = sb("xin", [128, 2, N])
    proj_b = sb("proj_b", [128, 2, N])
    proj_c = sb("proj_c", [128, 2, N])
    u = sb("u", [128, N])
    lnw = sb("lnw", [128, N])
    small = sb("small", [128, N])
    dd = sb("dd", [128, 2, N])
    parts = sb("parts", [128, 2, SPLITS, N], BF16)
    dA = sb("dA", [128, 4, 4, N])
    dBx = sb("dBx", [128, 4, 4, N])
    hst = sb("hst", [128, 4, 4, N])
    hc = sb("hc", [128, 2, 4, N])
    yt = sb("yt", [128, 2, N])

    dst_of = [x2, x3, None]
    src_of = [x1, x2, x3]

    def count(g, per, c):
        layer, k = g
        return k * per + (FIRST[layer] * per + c)

    def positive(v):
        return not isinstance(v, int) or v > 0

    def parity_count(g, par, per):
        layer, k = g
        return (k - par) * (per // 2) + (FIRST[layer] * (per // 2) + per)

    def groups(eng, emit):
        def nth(n):
            if n < 0 or n >= TOTAL:
                return None
            layer = max(i for i in range(LAYERS) if n >= FIRST[i])
            return (layer, n - FIRST[layer])
        for layer in range(LAYERS):
            G = GROUPS[layer]

            def static(k):
                n = FIRST[layer] + k
                emit(nth(n), n % 2, nth(n - 1), nth(n + 1), nth(n + 2))
            static(0)
            static(1)
            with eng.Fori(1, G // 2 - 1) as i:
                for j in range(2):
                    emit(*((layer, i * 2 + (j + d)) if d is not None else j for d in (0, None, -1, 1, 2)))
            static(G - 2)
            static(G - 1)
        return nth(TOTAL - 1)

    def bcast_e(ap, m):
        return ap.unsqueeze(1).to_broadcast([128, m, N])

    with nc.Block() as block:
        @block.sync
        def _(sp):
            def load_x(g, par, reader=None):
                layer, k = g
                G = 1 << layer
                src = src_of[layer][bass.ds(k * G, G), :, :].rearrange("g p l -> p g l")
                if reader is not None:
                    sp.wait_ge(s["skip_done"], count(reader, 1, 1))
                if layer > 0:
                    sp.wait_ge(s["y_out"], count((layer - 1, k * 2), 16, 32))
                sp.dma_start(xin[:, par, :].rearrange("p (g l) -> p g l", g=G), src).then_inc(s[f"x_in{par}"], 16)

            def store_parts(g, par):
                sp.wait_ge(s["m_g"], count(g, 2, 2))
                for r in range(4):
                    for b in range(2):
                        sp.dma_start(parts_dram[par, :, b, :, r, :].rearrange("q c n -> c q n"),
                                     parts[32 * r + b:32 * r + 32:2, :, :, :].rearrange("p a q n -> p (a q) n")
                                     ).then_inc(s["parts_out"], 16)
                sp.wait_ge(s["parts_out"], count(g, 128, 128))

            def load_rhs(g, par):
                layer, _ = g
                for q in range(QUARTERS):
                    c0, c1 = q * CH // QUARTERS, (q + 1) * CH // QUARTERS
                    arrived = s[f"rhs_in{q}"]
                    if positive(count(g, 32, 2 * c1 - 32)):
                        sp.wait_ge(s["pa_full"], count(g, 32, 2 * c1 - 32))

                    def rows(r, n):
                        return rhs[r:r + n, c0:c1, :, :].rearrange("r c k n -> r (c k n)")
                    def piece(ap):
                        return ap[:, c0:c1, :, :].rearrange("r c k n -> r (c k n)")
                    pd = parts_dram[par].rearrange("q b c k n -> (q b) c k n")
                    for j in range(SPLITS):
                        sp.dma_start(rows(DXROWS * j, DXROWS), piece(pd[0:DXROWS])).then_inc(arrived, 16)
                    sp.dma_start(rows(AROWS, 1), piece(io["reset_rows"][layer:layer + 1])).then_inc(arrived, 16)
                    sp.dma_start(rows(DX0, DXROWS), piece(pd[DXROWS:2 * DXROWS])).then_inc(arrived, 16)

            def store_y(g, par):
                layer, k = g
                if layer == LAYERS - 1:
                    dst = y3[bass.ds(k, 1), :, :].rearrange("g p l -> p (g l)")
                    src = yt[:, par, :]
                else:
                    G = 1 << layer
                    dst = dst_of[layer][bass.ds(k * G, G), :, :].rearrange("g p l -> p g l")
                    src = yt[:, par, 0:N // 2].rearrange("p (g l) -> p g l", g=G)
                sp.wait_ge(s["evac_done"], count(g, 1, 1))
                sp.dma_start(dst, src).then_inc(s["y_out"], 16)

            def emit(g, par, before, nxt, nxt2):
                if before is not None:
                    store_y(before, 1 - par)
                if nxt2 is not None:
                    load_x(nxt2, par, g)
                if nxt is not None:
                    store_parts(nxt, 1 - par)
                    load_rhs(nxt, 1 - par)

            load_x((0, 0), 0)
            load_x((0, 1), 1)
            store_parts((0, 0), 0)
            load_rhs((0, 0), 0)
            last = groups(sp, emit)
            store_y(last, 1)
            sp.wait_ge(s["y_out"], count(last, 16, 16))

        def pe_compact(pe, g, par, c):
            layer, _ = g
            def proj(w):
                return nc.tensor.matmul(psM[:, 0:N], w[layer][:], xin[:, par, :], start=True, stop=True)
            if c == 2:
                pe.wait_ge(s[f"x_in{par}"], parity_count(g, par, 16))
                if positive(count(g, 1, 0)):
                    pe.wait_ge(s["c_done"], count(g, 1, 0))
                proj(w_z).then_inc(s["z_ready"], 1)
            if c == 4:
                pe.wait_ge(s["m_a"], count(g, 7, 2))
                proj(w_b).then_inc(s["b_ready"], 1)
            if c == 6:
                pe.wait_ge(s["b_done"], count(g, 1, 1))
                proj(w_c).then_inc(s["c_ready"], 1)

        def act_compact(act, g, par, c):
            layer, _ = g
            a = nc.scalar.activation
            if c == 2:
                act.wait_ge(s["z_ready"], count(g, 1, 1))
                a(small[:], psM[:, 0:N], ACT.Abs, bias=bias_dt[:, layer:layer + 1]).then_inc(s["m_a"], 1)
                a(dd[:, 0, :], psM[:, 0:N], ACT.Relu, bias=bias_dt[:, layer:layer + 1]).then_inc(s["m_a"], 1)
            if c == 3:
                act.wait_ge(s["m_a"], count(g, 7, 1))
                a(u[:], small[:], ACT.Exp, scale=-1.0).then_inc(s["m_a"], 1)
                act.wait_ge(s["m_a"], count(g, 7, 3))
                a(small[:], u[:], ACT.Copy, bias=1.0, scale=-0.5).then_inc(s["m_a"], 1)
                a(lnw[:], u[:], ACT.Ln, bias=1.0).then_inc(s["m_a"], 1)
            if c == 4:
                act.wait_ge(s["b_ready"], count(g, 1, 1))
                a(proj_b[:, par, :], psM[:, 0:N], ACT.Copy).then_inc(s["b_done"], 1)
            if c == 6:
                act.wait_ge(s["c_ready"], count(g, 1, 1))
                a(proj_c[:, par, :], psM[:, 0:N], ACT.Copy).then_inc(s["c_done"], 1)
            if c == 8:
                act.wait_ge(s["m_v"], count(g, 5, 5))
                a(parts[:, :, 0, :], dd[:], ACT.Copy).then_inc(s["m_a"], 1)
            if c == 11:
                act.wait_ge(s["m_g"], count(g, 2, 1))
                a(parts[:, :, 1, :], dd[:], ACT.Copy).then_inc(s["m_a"], 1)

        def dve_compact(dve, g, par, c):
            v = nc.vector
            if c == 4:
                dve.wait_ge(s["m_a"], count(g, 7, 5))
                v.scalar_tensor_tensor(lnw[:], u[:], SMALL_U, lnw[:], ALU.is_ge, ALU.mult).then_inc(s["m_v"], 1)
                v.tensor_tensor(small[:], small[:], u[:], ALU.mult).then_inc(s["m_v"], 1)
            if c == 5:
                dve.wait_ge(s["m_v"], count(g, 5, 2))
                v.tensor_tensor(lnw[:], lnw[:], small[:], ALU.max).then_inc(s["m_v"], 1)
            if c == 6:
                dve.wait_ge(s["m_v"], count(g, 5, 3))
                v.tensor_tensor(dd[:, 0, :], lnw[:], dd[:, 0, :], ALU.add).then_inc(s["m_v"], 1)
            if c == 7:
                dve.wait_ge(s["m_v"], count(g, 5, 4))
                v.tensor_tensor(dd[:, 1, :], dd[:, 0, :], xin[:, par, :], ALU.mult).then_inc(s["m_v"], 1)

        def pool_compact(pool, g, par, c):
            p = nc.gpsimd
            if c == 6:
                pool.wait_ge(s["m_a"], count(g, 7, 6))
                p.tensor_tensor(dd[:], dd[:], parts[:, :, 0, :], ALU.subtract).then_inc(s["m_g"], 1)
            if c == 9:
                pool.wait_ge(s["m_a"], count(g, 7, 7))
                p.tensor_tensor(parts[:, :, 2, :], dd[:], parts[:, :, 1, :],
                                ALU.subtract).then_inc(s["m_g"], 1)

        @block.tensor
        def _(pe):
            mm = nc.tensor.matmul

            def spread_dx(g, c, hf):
                if c % (CH // QUARTERS) == 0 and hf == 0:
                    pe.wait_ge(s[f"rhs_in{c * QUARTERS // CH}"], count(g, 80, 80))
                if positive(count(g, 32, 2 * c + hf - 1)):
                    pe.wait_ge(s["dbx_done"], count(g, 32, 2 * c + hf - 1))
                for q in range(2):
                    ins = mm(psX[hf][:, q, 0:N], w_dx[0:KR], rhs[0:KR, c, 2 * hf + q, :], start=True, stop=True)
                ins.then_inc(s["px_full"], 1)

            def spread_a(g, c, hf):
                layer, _ = g
                if positive(count(g, 32, 2 * c + hf)):
                    pe.wait_ge(s["exp_done"], count(g, 32, 2 * c + hf))
                for q in range(2):
                    e = c + CH * (2 * hf + q)
                    ins = mm(psA[:, q, 0:N], w_a[layer][0:KR, e, :, :], rhs[0:KR, c, 2 * hf + q, :],
                             start=True, stop=True)
                ins.then_inc(s["pa_full"], 1)

            def reduce(g, par, c):
                layer, _ = g
                if c == 0:
                    if positive(count(g, 1, 0)):
                        pe.wait_ge(s["evac_done"], count(g, 1, 0))
                    mm(psY[:, 0:N], w_d[layer][:], xin[:, par, :], start=True, stop=False,
                       skip_group_check=True).then_inc(s["skip_done"], 1)
                pe.wait_ge(s["hc_done"], count(g, 16, c + 1))
                for r in range(4):
                    ins = mm(psY[32 * r:32 * r + 32, 0:N], sel[:, c, :], hc[:, c % 2, r, :],
                             start=False, stop=c == CH - 1, skip_group_check=True)
                ins.then_inc(s["red_done"], 1)

            def emit(g, par, before, nxt, nxt2):
                for c in range(CH):
                    for hf in range(2):
                        spread_dx(g, c, hf)
                        spread_a(g, c, hf)
                        if hf == 1:
                            continue
                        if c >= LAG:
                            reduce(g, par, c - LAG)
                        elif before is not None:
                            reduce(before, 1 - par, CH + c - LAG)
                    if nxt is not None:
                        pe_compact(pe, nxt, 1 - par, c)

            for c in range(CH):
                pe_compact(pe, (0, 0), 0, c)
            last = groups(pe, emit)
            for c in range(CH - LAG, CH):
                reduce(last, 1, c)

        @block.scalar
        def _(act):
            def decay(g, c):
                if positive(count(g, 16, c - 2)):
                    act.wait_ge(s["scan_done"], count(g, 16, c - 2))
                for hf in range(2):
                    act.wait_ge(s["pa_full"], count(g, 32, 2 * c + hf + 1))
                    nc.scalar.activation(dA[:, c % 4, 2 * hf:2 * hf + 2, :], psA[:, :, 0:N],
                                         ACT.Exp).then_inc(s["exp_done"], 1)

            def emit(g, par, before, nxt, nxt2):
                for c in range(CH):
                    decay(g, c)
                    if nxt is not None:
                        act_compact(act, nxt, 1 - par, c)

            for c in range(CH):
                act_compact(act, (0, 0), 0, c)
            groups(act, emit)

        @block.vector
        def _(dve):
            v = nc.vector

            def scan(g, c):
                dve.wait_ge(s["exp_done"], count(g, 32, 2 * c + 2))
                dve.wait_ge(s["dbx_done"], count(g, 32, 2 * c + 2))
                if positive(count(g, 16, c - 3)):
                    dve.wait_ge(s["hc_done"], count(g, 16, c - 3))
                v.tensor_tensor_scan(hst[:, c % 4, :, :].rearrange("p e n -> p (e n)"),
                                     dA[:, c % 4, :, :].rearrange("p e n -> p (e n)"),
                                     dBx[:, c % 4, :, :].rearrange("p e n -> p (e n)"),
                                     0.0, ALU.mult, ALU.add).then_inc(s["scan_done"], 1)

            def evac(g, par):
                layer, _ = g
                dve.wait_ge(s["red_done"], count(g, 16, 16))
                if layer == LAYERS - 1:
                    v.tensor_scalar(yt[:, par, :], psY[:, 0:N], 2.0, None, ALU.mult).then_inc(s["evac_done"], 1)
                else:
                    v.tensor_reduce(yt[:, par, 0:N // 2], psY[:, 0:N].rearrange("p (l two) -> p l two", two=2),
                                    AX.X, ALU.add).then_inc(s["evac_done"], 1)

            def emit(g, par, before, nxt, nxt2):
                for c in range(CH):
                    if positive(count(g, 16, c - 3)):
                        dve.wait_ge(s["scan_done"], count(g, 16, c - 3))
                    for hf in range(2):
                        if c == 0 and hf == 0:
                            dve.wait_ge(s["b_done"], count(g, 1, 1))
                        dve.wait_ge(s["px_full"], count(g, 32, 2 * c + hf + 1))
                        v.tensor_tensor(dBx[:, c % 4, 2 * hf:2 * hf + 2, :], psX[hf][:, :, 0:N],
                                        bcast_e(proj_b[:, par, :], 2), ALU.mult).then_inc(s["dbx_done"], 1)
                    if c == LAG - 1 and before is not None:
                        evac(before, 1 - par)
                    if c > 0:
                        scan(g, c - 1)
                    elif before is not None:
                        scan(before, CH - 1)
                    if nxt is not None:
                        dve_compact(dve, nxt, 1 - par, c)

            for c in range(CH):
                dve_compact(dve, (0, 0), 0, c)
            last = groups(dve, emit)
            scan(last, CH - 1)
            evac(last, 1)

        @block.gpsimd
        def _(pool):
            def emit(g, par, before, nxt, nxt2):
                for c in range(CH):
                    if c == 0:
                        pool.wait_ge(s["c_done"], count(g, 1, 1))
                    pool.wait_ge(s["scan_done"], count(g, 16, c + 1))
                    if positive(count(g, 16, c - 1)):
                        pool.wait_ge(s["red_done"], count(g, 16, c - 1))
                    nc.gpsimd.tensor_tensor(hc[:, c % 2, :, :], hst[:, c % 4, :, :],
                                            bcast_e(proj_c[:, par, :], 4), ALU.mult).then_inc(s["hc_done"], 1)
                    if nxt is not None:
                        pool_compact(pool, nxt, 1 - par, c)

            for c in range(CH):
                pool_compact(pool, (0, 0), 0, c)
            groups(pool, emit)


LT = LEN3
GP = 4
SEQS = 2 * GP
E_FFN = 16
EPS = 1e-5
STEPS = E_FFN


def attention_ffn_stage(nc, io, out):
    with ExitStack() as ctx:
        def sb(name, shape, dt=F32):
            return ctx.enter_context(nc.sbuf_tensor(name, shape, dt))

        def ps(name, shape, dt=F32):
            return ctx.enter_context(nc.psum_tensor(name, shape, dt))

        sems = {}

        def sem(name):
            if name not in sems:
                sems[name] = ctx.enter_context(nc.semaphore("f_" + name))
            return sems[name]

        w = {n: sb("f_" + n, list(io[n].shape)) for n in (
            "wq_t", "wk_t", "wv_t", "gate_t", "bq_c", "bk_c", "w1_t", "b1_t", "w2_t", "b2_t", "ident", "halves",
            "halves_g", "halves_b", "order")}
        rows = {n: sb("f_" + n, [LT, io[n].shape[1]]) for n in ("bv_r", "gateb_r", "gamma_r", "beta_r")}
        eps_c = sb("f_eps", [128, 1])
        feat = sb("f_feat", [128, N])
        hid = sb("f_hid", [LT, 2, GP, D])
        cen = sb("f_cen", [LT, SEQS, D])
        sq = sb("f_sq", [LT, SEQS, D])
        stat = sb("f_stat", [LT, 4, SEQS])
        xn = sb("f_xn", [LT, GP, 2, D])
        xn2 = [sb(f"f_xn2_{i}", [LT, GP, 2, D]) for i in range(2)]
        xn2_t = [sb(f"f_xn2_t{i}", [128, N]) for i in range(2)]
        xn_t = sb("f_xn_t", [128, N])
        q_t = sb("f_q_t", [128, N])
        k_t = sb("f_k_t", [128, N])
        val = sb("f_val", [LT, GP, 2, D])
        peak = sb("f_peak", [LT, 2, GP])
        prob = sb("f_prob", [LT, 2, GP, LT])
        prob_t = sb("f_prob_t", [LT, 2, N])
        den = sb("f_den", [LT, 2, 2, GP])
        att = sb("f_att", [LT, 2, GP, D])
        hid2 = [sb(f"f_hid2_{i}", [LT, 2, GP, D]) for i in range(2)]
        start = [sb(f"f_start{i}", [LT, SEQS, D]) for i in range(2)]
        logit = sb("f_logit", [LT, SEQS, E_FFN])
        pick = sb("f_pick", [LT, 2, SEQS, E_FFN])
        code = sb("f_code", [LT, SEQS, E_FFN])
        top = sb("f_top", [LT, 6, SEQS])
        gates = [sb(f"f_gates{i}", [LT, SEQS, E_FFN]) for i in range(2)]
        fin_n = sb("f_fin_n", [LT, SEQS, D])
        fin_a = sb("f_fin_a", [LT, SEQS, D])
        gates_t = sb("f_gates_t", [2 * E_FFN, N])
        hidden = sb("f_hidden", [128, 2, 2, N])
        scaled = sb("f_scaled", [LT, 2, SEQS, D])
        acc = [sb(f"f_acc{i}", [LT, SEQS, D]) for i in range(2)]
        res = sb("f_res", [LT, 2, GP, D])
        fin_c = sb("f_fin_c", [LT, SEQS, D])
        fin_s = sb("f_fin_s", [LT, 4, SEQS])

        pT = ps("f_pT", [128, BANK])
        pB = ps("f_pB", [128, BANK])
        pH = ps("f_pH", [128, 2, BANK])
        pF = [ps(f"f_pF{i}", [128, BANK]) for i in range(2)]
        pE = ps("f_pE", [128, BANK])
        pG = ps("f_pG", [128, BANK])

        with nc.Block() as block:
            @block.sync
            def _(sp):
                for n, tile in {**w, **rows}.items():
                    src = io[n] if n in w else io[n].partition_broadcast(LT).rearrange("p a c -> p (a c)")
                    sp.dma_start(tile[:], src).then_inc(sem("weights"), 16)
                sp.wait_ge(sem("weights"), 16 * (len(w) + len(rows)))

            @block.vector
            def _(dve):
                nc.vector.memset(eps_c[:], EPS).then_inc(sem("eps"), 1)
                dve.wait_ge(sem("weights"), 16 * (len(w) + len(rows)))
                for n in ("wq_t", "wk_t", "wv_t"):
                    nc.vector.tensor_tensor(w[n][:], w[n][:], w["halves"][:], ALU.mult).then_inc(sem("masked"), 1)
                nc.vector.tensor_tensor(w["gate_t"][:], w["gate_t"][:], w["halves_g"][:],
                                        ALU.mult).then_inc(sem("masked"), 1)
                nc.vector.tensor_tensor(w["b2_t"][:], w["b2_t"][:], w["halves_b"][:],
                                        ALU.mult).then_inc(sem("masked"), 1)

        def positive(v):
            return not isinstance(v, int) or v > 0

        def pipeline(eng, attend, expert, finish):
            last = GROUPS[-1] - 1
            for st in range(STEPS):
                attend(0, 0, st)

            def group(before, k, par, nxt):
                for x in range(E_FFN):
                    expert(k, par, x)
                    if nxt is not None:
                        attend(nxt, 1 - par, x)
                    if before is not None:
                        finish(before, 1 - par, x)
            group(None, 0, 0, 1)
            group(0, 1, 1, 2)
            with eng.Fori(1, GROUPS[-1] // 2 - 1) as i:
                for par in range(2):
                    group(i * 2 + (par - 1), i * 2 + par, par, i * 2 + (par + 1))
            group(last - 2, last - 1, 0, last)
            group(last - 1, last, 1, None)
            for st in range(STEPS):
                finish(last, 1, st)

        def wide(ap, n):
            return ap.unsqueeze(3).to_broadcast([LT, ap.shape[1], ap.shape[2], n])

        def nothing(*_):
            pass

        with nc.Block() as block:
            @block.sync
            def _(sp):
                def attend(k, par, st):
                    if st == 0:
                        src = io["y3"][bass.ds(k, 1), :, :].rearrange("a p n -> p (a n)")
                        if positive(k):
                            sp.wait_ge(sem("tokens"), k)
                        sp.dma_start(feat[:], src).then_inc(sem("feat"), 16)

                def finish(k, par, st):
                    if st == 7:
                        dst = out[bass.ds(k * SEQS, SEQS), :, :].rearrange("(g b) l e -> b l g e", b=2)
                        sp.wait_ge(sem("res"), k + 1)
                        for b in range(2):
                            sp.dma_start(dst[b], res[:, b, :, :]).then_inc(sem("stored"), 16)
                pipeline(sp, attend, nothing, finish)
                sp.wait_ge(sem("stored"), 32 * GROUPS[-1])

            @block.tensor
            def _(pe):
                mm, tr = nc.tensor.matmul, nc.tensor.transpose
                ident = w["ident"]

                def to_features(src):
                    for g in range(GP):
                        ins = tr(pB[:, g * LT:(g + 1) * LT], src[:, g, :, :].rearrange("p b e -> p (b e)"),
                                 ident[0:LT, 0:LT])
                    return ins

                def attend(k, par, st):
                    if st == 0:
                        pe.wait_ge(sem("feat"), k * 16 + 16)
                        for g in range(GP):
                            ins = tr(pT[0:LT, g * 128:(g + 1) * 128], feat[:, g * LT:(g + 1) * LT], ident[:])
                        ins.then_inc(sem("tokens"), 1)
                    if st == 3:
                        pe.wait_ge(sem("xn"), k + 1)
                        to_features(xn).then_inc(sem("xn_ps"), 1)
                    if st == 4:
                        pe.wait_ge(sem("xn_t"), k + 1)
                        mm(pT[:, 0:N], w["wq_t"][:], xn_t[:], start=True, stop=True)
                        mm(pG[:, 0:N], w["wk_t"][:], xn_t[:], start=True, stop=True).then_inc(sem("qk_ps"), 1)
                        for g in range(GP):
                            ins = mm(pE[0:LT, g * 128:(g + 1) * 128], xn_t[:, g * LT:(g + 1) * LT], w["wv_t"][:],
                                     start=True, stop=True)
                        ins.then_inc(sem("v_ps"), 1)
                    if st == 5:
                        pe.wait_ge(sem("qk"), k * 2 + 2)
                        for b in range(2):
                            for g in range(GP):
                                cols = slice(g * LT, (g + 1) * LT)
                                ins = mm((pT, pG)[b][0:LT, cols], q_t[64 * b:64 * b + 64, cols],
                                         k_t[64 * b:64 * b + 64, cols], start=True, stop=True)
                        ins.then_inc(sem("scores"), 1)
                    if st == 7:
                        pe.wait_ge(sem("prob"), k + 1)
                        for b in range(2):
                            for g in range(GP):
                                ins = tr((pB, pT)[b][0:LT, g * LT:(g + 1) * LT], prob[:, b, g, :], ident[0:LT, 0:LT])
                        ins.then_inc(sem("prob_ps"), 1)
                    if st == 8:
                        pe.wait_ge(sem("prob_t"), k * 2 + 2)
                        pe.wait_ge(sem("val"), k + 1)
                        for b in range(2):
                            for g in range(GP):
                                j = b * GP + g
                                ins = mm(pE[0:LT, j * D:(j + 1) * D], prob_t[:, b, g * LT:(g + 1) * LT],
                                         val[:, g, b, :], start=True, stop=True)
                        ins.then_inc(sem("att_ps"), 1)
                    if st == 11:
                        pe.wait_ge(sem("xn2"), k + 1)
                        to_features(xn2[par]).then_inc(sem("xn2_ps"), 1)
                    if st == 12:
                        pe.wait_ge(sem("xn2_t"), k + 1)
                        for g in range(GP):
                            ins = mm(pG[0:LT, g * 32:(g + 1) * 32], xn2_t[par][:, g * LT:(g + 1) * LT],
                                     w["gate_t"][:], start=True, stop=True)
                        ins.then_inc(sem("logit_ps"), 1)
                    if st == 14:
                        pe.wait_ge(sem("gates"), k + 1)
                        for g in range(GP):
                            ins = tr(pT[0:2 * E_FFN, g * LT:(g + 1) * LT],
                                     gates[par][:, 2 * g:2 * g + 2, :].rearrange("p b x -> p (b x)"),
                                     ident[0:LT, 0:LT])
                        ins.then_inc(sem("gates_ps"), 1)
                    if st == 15:
                        pe.wait_ge(sem("gates_t"), k + 1)
                        for g in range(GP):
                            ins = mm(pE[0:LT, g * 128:(g + 1) * 128], gates_t[:, g * LT:(g + 1) * LT],
                                     w["b2_t"][:], start=True, stop=True)
                        ins.then_inc(sem("bias2_ps"), 1)

                def first(k, par, x):
                    if positive(k * E_FFN + x):
                        pe.wait_ge(sem("hidden"), k * E_FFN + x)
                    if x == 0:
                        pe.wait_ge(sem("xn2_t"), k + 1)
                    for b in range(2):
                        ins = mm(pH[:, b, 0:N], w["w1_t"][64 * b:64 * b + 64, x, :],
                                 xn2_t[par][64 * b:64 * b + 64, :], start=True, stop=True)
                    ins.then_inc(sem("hidden_ps"), 1)

                def expert(k, par, x):
                    if x == 0:
                        first(k, par, 0)
                    if x + 1 < E_FFN:
                        first(k, par, x + 1)
                    pe.wait_ge(sem("hidden"), k * E_FFN + (x + 1))
                    if positive(k * E_FFN + (x - 1)):
                        pe.wait_ge(sem("scaled"), k * E_FFN + (x - 1))
                    for g in range(GP):
                        for b in range(2):
                            j = 2 * g + b
                            ins = mm(pF[x % 2][0:LT, j * D:(j + 1) * D],
                                     hidden[:, x % 2, b, g * LT:(g + 1) * LT], w["w2_t"][:, x, :],
                                     start=True, stop=True)
                    ins.then_inc(sem("expert_ps"), 1)
                pipeline(pe, attend, expert, nothing)

            @block.scalar
            def _(act):
                a = nc.scalar.activation

                def rstd(k, which, st):
                    act.wait_ge(sem("var" + which), k + 1)
                    a(st[:, 3, :], st[:, 1, :], ACT.Ln, bias=eps_c[0:LT, :]).then_inc(sem("log" + which), 1)
                    act.wait_ge(sem("log" + which), k + 1)
                    a(st[:, 2, :], st[:, 3, :], ACT.Exp, scale=-0.5).then_inc(sem("rstd" + which), 1)

                def attend(k, par, st):
                    if st == 2:
                        rstd(k, "1", stat)
                    if st == 7:
                        act.wait_ge(sem("shifted"), k * 2 + 2)
                        a(prob[:], prob[:], ACT.Exp, scale=float(D) ** -0.5).then_inc(sem("prob"), 1)
                    if st == 10:
                        rstd(k, "2", stat)
                    if st == 13:
                        act.wait_ge(sem("gap"), k + 1)
                        a(top[:, 4, :], top[:, 2, :], ACT.Exp).then_inc(sem("ratio"), 1)

                def expert(k, par, x):
                    act.wait_ge(sem("hidden_ps"), k * E_FFN + (x + 1))
                    if positive(k * E_FFN + (x - 1)):
                        act.wait_ge(sem("expert_ps"), k * E_FFN + (x - 1))
                    a(hidden[:, x % 2, :, :], pH[:, :, 0:N], ACT.Relu, bias=w["b1_t"][:, x:x + 1]
                      ).then_inc(sem("hidden"), 1)

                def finish(k, par, st):
                    if st == 6:
                        rstd(k, "3", fin_s)
                pipeline(act, attend, expert, finish)

            @block.vector
            def _(dve):
                v = nc.vector
                ATTEND_STEPS, FINISH_STEPS = 31, 6
                made = {}

                def chained(name, k, per):
                    def then(ins):
                        made[name] += 1
                        ins.then_inc(sem(name), 1)
                        dve.wait_ge(sem(name), k * per + made[name])
                    return then

                def norm_sums(then, which, rows_in, centred, st):
                    mean = st[:, 0, :].unsqueeze(2).to_broadcast([LT, SEQS, D])
                    then(v.tensor_reduce(st[:, 0, :], rows_in, AX.X, ALU.add))
                    then(v.scalar_tensor_tensor(centred[:], mean, -1.0 / D, rows_in, ALU.mult, ALU.add))
                    then(v.scalar_tensor_tensor(sq[:], centred[:], 1.0 / D, centred[:], ALU.mult, ALU.mult))
                    v.tensor_reduce(st[:, 1, :], sq[:], AX.X, ALU.add).then_inc(sem("var" + which), 1)

                def normed(k, which, dst):
                    dve.wait_ge(sem("rstd" + which), k + 1)
                    return v.tensor_tensor(dst.rearrange("p g b e -> p b g e"),
                                           cen[:].rearrange("p (b g) e -> p b g e", b=2),
                                           wide(stat[:, 2, :].rearrange("p (b g) -> p b g", b=2), D), ALU.mult)

                def over(ap):
                    return ap.unsqueeze(2).to_broadcast([LT, SEQS, E_FFN])

                def attend(k, par, st):
                    if st == 0:
                        made["attend_step"] = 0
                    then = chained("attend_step", k, ATTEND_STEPS)
                    lg = logit[:]
                    if st == 0:
                        dve.wait_ge(sem("tokens"), k + 1)
                        then(v.tensor_copy(hid[:], pT[0:LT, :].rearrange("p (g e b) -> p b g e", g=GP, b=2)))
                        norm_sums(then, "1", hid[:].rearrange("p b g e -> p (b g) e"), cen, stat)
                    if st == 2:
                        normed(k, "1", xn[:]).then_inc(sem("xn"), 1)
                    if st == 3:
                        dve.wait_ge(sem("xn_ps"), k + 1)
                        v.tensor_copy(xn_t[:], pB[:, 0:N]).then_inc(sem("xn_t"), 1)
                    if st == 4:
                        dve.wait_ge(sem("qk_ps"), k + 1)
                        v.tensor_scalar(q_t[:], pT[:, 0:N], w["bq_c"][:, 0:1], None, ALU.add).then_inc(sem("qk"), 1)
                        v.tensor_scalar(k_t[:], pG[:, 0:N], w["bk_c"][:, 0:1], None, ALU.add).then_inc(sem("qk"), 1)
                        dve.wait_ge(sem("v_ps"), k + 1)
                        v.tensor_tensor(val[:].rearrange("p g b e -> p g (b e)"),
                                        pE[0:LT, :].rearrange("p (g m) -> p g m", g=GP),
                                        rows["bv_r"][:].unsqueeze(1).to_broadcast([LT, GP, 128]),
                                        ALU.add).then_inc(sem("val"), 1)
                    if st == 5:
                        dve.wait_ge(sem("scores"), k + 1)
                        for b in range(2):
                            s3 = (pT, pG)[b][0:LT, 0:N].rearrange("p (g t) -> p g t", g=GP)
                            then(v.tensor_reduce(peak[:, b, :], s3, AX.X, ALU.max))
                            v.tensor_tensor(prob[:, b, :, :], s3,
                                            peak[:, b, :].unsqueeze(2).to_broadcast([LT, GP, LT]),
                                            ALU.subtract).then_inc(sem("shifted"), 1)
                    if st == 7:
                        dve.wait_ge(sem("prob_ps"), k + 1)
                        for b in range(2):
                            v.tensor_copy(prob_t[:, b, :], (pB, pT)[b][0:LT, 0:N]).then_inc(sem("prob_t"), 1)
                        dve.wait_ge(sem("prob"), k + 1)
                        then(v.tensor_reduce(den[:, 0, :, :], prob[:], AX.X, ALU.add))
                        then(v.reciprocal(den[:, 1, :, :], den[:, 0, :, :]))
                    if st == 8:
                        dve.wait_ge(sem("att_ps"), k + 1)
                        then(v.tensor_tensor(att[:], pE[0:LT, :].rearrange("p (b g e) -> p b g e", b=2, g=GP),
                                             wide(den[:, 1, :, :], D), ALU.mult))
                        then(v.tensor_tensor(hid2[par][:], hid[:], att[:], ALU.add))
                        norm_sums(then, "2", hid2[par][:].rearrange("p b g e -> p (b g) e"), cen, stat)
                    if st == 10:
                        normed(k, "2", xn2[par][:]).then_inc(sem("xn2"), 1)
                    if st == 11:
                        dve.wait_ge(sem("xn2_ps"), k + 1)
                        v.tensor_copy(xn2_t[par][:], pB[:, 0:N]).then_inc(sem("xn2_t"), 1)
                    order = w["order"][0:LT, :].unsqueeze(1).to_broadcast([LT, SEQS, E_FFN])
                    if st == 12:
                        dve.wait_ge(sem("logit_ps"), k + 1)
                        then(v.tensor_tensor(lg.rearrange("p (g b) x -> p g (b x)", g=GP),
                                             pG[0:LT, 0:GP * 32].rearrange("p (g m) -> p g m", g=GP),
                                             rows["gateb_r"][:].unsqueeze(1).to_broadcast([LT, GP, 32]), ALU.add))
                        for i in range(2):
                            then(v.tensor_reduce(top[:, i, :], lg, AX.X, ALU.max))
                            then(v.tensor_tensor(code[:], lg, over(top[:, i, :]), ALU.is_equal))
                            then(v.tensor_tensor(code[:], code[:], order, ALU.mult))
                            then(v.tensor_reduce(top[:, 5, :], code[:], AX.X, ALU.max))
                            then(v.tensor_tensor(pick[:, i, :, :], code[:], over(top[:, 5, :]), ALU.is_equal))
                            if i == 0:
                                then(v.tensor_scalar(code[:], pick[:, 0, :, :], -3e38, None, ALU.mult))
                                then(v.tensor_tensor(lg, lg, code[:], ALU.add))
                        v.tensor_tensor(top[:, 2, :], top[:, 1, :], top[:, 0, :], ALU.subtract
                                        ).then_inc(sem("gap"), 1)
                    if st == 13:
                        dve.wait_ge(sem("ratio"), k + 1)
                        then(v.tensor_scalar(top[:, 5, :], top[:, 4, :], 1.0, None, ALU.add))
                        then(v.reciprocal(top[:, 2, :], top[:, 5, :]))
                        then(v.tensor_tensor(top[:, 3, :], top[:, 4, :], top[:, 2, :], ALU.mult))
                        then(v.tensor_tensor(gates[par][:], pick[:, 0, :, :], over(top[:, 2, :]), ALU.mult))
                        then(v.tensor_tensor(code[:], pick[:, 1, :, :], over(top[:, 3, :]), ALU.mult))
                        v.tensor_tensor(gates[par][:], gates[par][:], code[:], ALU.add).then_inc(sem("gates"), 1)
                    if st == 14:
                        dve.wait_ge(sem("gates_ps"), k + 1)
                        v.tensor_copy(gates_t[:], pT[0:2 * E_FFN, 0:N]).then_inc(sem("gates_t"), 1)
                    if st == 15:
                        dve.wait_ge(sem("bias2_ps"), k + 1)
                        v.tensor_tensor(start[par][:], xn2[par][:].rearrange("p g b e -> p (g b) e"),
                                        pE[0:LT, :].rearrange("p (j e) -> p j e", j=SEQS),
                                        ALU.add).then_inc(sem("start"), 1)
                        assert made["attend_step"] == ATTEND_STEPS, made

                def expert(k, par, x):
                    dve.wait_ge(sem("expert_ps"), k * E_FFN + (x + 1))
                    if x == 0:
                        dve.wait_ge(sem("gates"), k + 1)
                    if positive(k * E_FFN + (x - 1)):
                        dve.wait_ge(sem("summed"), k * E_FFN + (x - 1))
                    v.tensor_tensor(scaled[:, x % 2, :, :], pF[x % 2][0:LT, :].rearrange("p (j e) -> p j e", j=SEQS),
                                    gates[par][:, :, x:x + 1].to_broadcast([LT, SEQS, D]),
                                    ALU.mult).then_inc(sem("scaled"), 1)

                def finish(k, par, st):
                    if st == 0:
                        made["finish_step"] = 0
                    then = chained("finish_step", k, FINISH_STEPS)
                    if st == 4:
                        dve.wait_ge(sem("summed"), k * E_FFN + E_FFN)
                        norm_sums(then, "3", acc[par][:], fin_c, fin_s)
                    if st == 6:
                        dve.wait_ge(sem("rstd3"), k + 1)
                        then(v.tensor_tensor(fin_n[:], fin_c[:],
                                             fin_s[:, 2, :].unsqueeze(2).to_broadcast([LT, SEQS, D]), ALU.mult))
                        then(v.tensor_tensor(fin_a[:], fin_n[:],
                                             rows["gamma_r"][:].unsqueeze(1).to_broadcast([LT, SEQS, D]), ALU.mult))
                        then(v.tensor_tensor(fin_a[:], fin_a[:],
                                             rows["beta_r"][:].unsqueeze(1).to_broadcast([LT, SEQS, D]), ALU.add))
                        if positive(k * 32):
                            dve.wait_ge(sem("stored"), k * 32)
                        v.tensor_tensor(res[:].rearrange("p b g e -> p g b e"),
                                        fin_a[:].rearrange("p (g b) e -> p g b e", g=GP),
                                        hid2[par][:].rearrange("p b g e -> p g b e"), ALU.add).then_inc(sem("res"), 1)
                        assert made["finish_step"] == FINISH_STEPS, made
                pipeline(dve, attend, expert, finish)

            @block.gpsimd
            def _(pool):
                def expert(k, par, x):
                    if x == 0:
                        pool.wait_ge(sem("start"), k + 1)
                    pool.wait_ge(sem("scaled"), k * E_FFN + (x + 1))
                    if positive(k * E_FFN + x):
                        pool.wait_ge(sem("summed"), k * E_FFN + x)
                    nc.gpsimd.tensor_tensor(acc[par][:], start[par][:] if x == 0 else acc[par][:],
                                            scaled[:, x % 2, :, :], ALU.add).then_inc(sem("summed"), 1)
                pipeline(pool, nothing, expert, nothing)


def tower(nc, io, out):
    with ExitStack() as ctx:
        ssm_stage(nc, ctx, io)
    attention_ffn_stage(nc, io, out)


def _layouts(inputs):
    f32, bf16 = np.float32, mybir.dt.np(BF16)
    lane = np.arange(128)
    channel, seq = lane // 2, lane % 2
    seq_s, state = lane // 64, lane % 64
    x = inputs["x"][:, :N].reshape(PAIRS, 2, N, D).transpose(0, 3, 1, 2).reshape(PAIRS, 128, N)
    w_dbc = inputs["L0_tok_W_dbc"]
    got = {
        "x": x, "w0": w_dbc[:, 0, :][:, channel].T, "dcol": inputs["L0_tok_D"][:, channel].T,
        "bdt": inputs["L0_tok_b_dt"][:, channel].T,
        "wb": w_dbc[:, 1:1 + NST, :][:, state][:, :, channel].transpose(2, 0, 1),
        "wc": w_dbc[:, 1 + NST:, :][:, state][:, :, channel].transpose(2, 0, 1),
        "wdt": inputs["L0_tok_W_dt"][:, channel, 0], "A_log": inputs["L0_tok_A_log"],
        "bq_c": inputs["L0_attn_bq"][state][:, None], "bk_c": inputs["L0_attn_bk"][state][:, None],
        "bv_r": inputs["L0_attn_bv"][state][None], "gateb_r": inputs["L0_ffn_gate_b"][np.arange(32) % 16][None],
        "gamma_r": inputs["L0_ffn_gamma"][None], "beta_r": inputs["L0_ffn_beta"][None],
        "gate_t": inputs["L0_ffn_gate_w"][state][:, np.arange(32) % 16],
        "w1_t": inputs["L0_ffn_w1"].transpose(1, 0, 2)[state], "b1_t": inputs["L0_ffn_b1"].T,
        "w2_t": inputs["L0_ffn_w2"].transpose(1, 0, 2), "b2_t": inputs["L0_ffn_b2"][np.arange(32) % 16][:, state],
    }
    for n in "qkv":
        got[f"w{n}_t"] = inputs[f"L0_attn_W{n}"].T[state][:, state]
    got["mask_z"] = np.equal.outer(seq, seq).astype(f32)
    got["mask_n"] = np.equal.outer(seq, seq_s).astype(f32)
    got["halves"] = np.equal.outer(seq_s, seq_s).astype(f32)
    got["halves_g"] = np.equal.outer(seq_s, np.arange(32) // 16).astype(f32)
    got["halves_b"] = np.equal.outer(np.arange(32) // 16, seq_s).astype(f32)
    got["ident"] = np.eye(128, dtype=f32)
    got["order"] = np.tile(np.arange(16, 0, -1, dtype=f32), (128, 1))
    sel = np.zeros((128, CH, 32), f32)
    for c in range(CH):
        sel[:64, c, 2 * c] = 1
        sel[64:, c, 2 * c + 1] = 1
    got["sel"] = sel
    ones_dx = np.zeros((DXROWS, 2, NST), bf16)
    for r in range(DXROWS):
        ones_dx[r, r % 2] = 1
    got["ones_dx"] = ones_dx
    got["ones_row"] = np.ones((1, D * 2 * NST), bf16)
    reset = np.zeros((LAYERS, CH, 4, N), bf16)
    for i, length in enumerate(LENS):
        reset[i, :, :, ::length] = RESET
    got["reset_rows"] = reset
    return got


def kernel(**inputs):
    import concourse.bacc as _bacc
    from concourse.bass_utils import run_bass_kernel_spmd as _run

    nc = _bacc.Bacc("TRN2", target_bir_lowering=False, num_devices=1)
    arrays, io = {}, {}
    for name, a in _layouts({k: np.asarray(v) for k, v in inputs.items()}).items():
        a = np.ascontiguousarray(a)
        arrays[f"in_{name}_dram"] = a
        io[name] = nc.dram_tensor(f"in_{name}_dram", a.shape, mybir.dt.from_np(a.dtype), kind="ExternalInput").ap()
    for name, shape, dt in (("x2", [PAIRS, 128, N // 2], F32), ("x3", [PAIRS, 128, N // 4], F32),
                            ("y3", [GROUPS[-1], 128, N], F32), ("a_dram", [LAYERS, SPLITS, 2, D, 2 * NST], BF16),
                            ("parts_dram", [2, 2 * SPLITS, 2, CH, 4, N], BF16)):
        io[name] = nc.dram_tensor(f"{name}_dram", shape, dt).ap()
    out = nc.dram_tensor("out_dram", [BATCH, LEN3, D], F32, kind="ExternalOutput").ap()
    tower(nc, io, out)
    r = _run(nc, [arrays], core_ids=[0])
    return r.results[0]["out_dram"]
```
